# Optimizing a Trainium2 kernel written in Bass

```python
import numpy as np
import jax
import jax.numpy as jnp

def _softmax(x, axis=-1):
    return jax.nn.softmax(x, axis=axis)
def _gelu(x):
    return jax.nn.gelu(x, approximate=True)
def _silu(x):
    return jax.nn.silu(x)
def _sigmoid(x):
    return jax.nn.sigmoid(x)
def _layernorm(x, axis=-1, eps=1e-5):
    m = jnp.mean(x, axis=axis, keepdims=True)
    v = jnp.var(x, axis=axis, keepdims=True)
    return (x - m) / jnp.sqrt(v + eps)
def _scatter_add(tgt, idx, src, axis=0):
    return tgt.at[idx].add(src)
def _segment_sum(src, seg, n):
    return jax.ops.segment_sum(src, seg, n)

kernel_name = 'mk_conv_preact_d4_conv_nhwc32_b369cd'

def setup_inputs(seed: int = 0):
    np.random.seed(seed)
    _w = jnp.asarray
    def _rec_inputs():
        import jax
        import jax.numpy as jnp
        _gk = jax.random.key(seed)
        x = 0.0003368 + 1 * jax.random.normal(jax.random.fold_in(_gk, 1), (16, 224, 224, 32), jnp.float32)
        return x
    x = _rec_inputs()
    def _L0_conv_setup():
        import jax, jax.numpy as jnp
        import numpy as np
        from jax import lax
        MAX_SCALE = 4
        SCALES = [2 ** i for i in range(1, MAX_SCALE + 1)]
        EPS_K = 1e-07
        BN_EPS = 0.001

        def sample_min_max_scaling(x):
            mn = jnp.min(x, axis=(1, 2, 3), keepdims=True)
            mx = jnp.max(x, axis=(1, 2, 3), keepdims=True)
            return (x - mn) / (mx - mn + EPS_K)

        def box_sum(x, r):
            c = x.shape[-1]
            kernel = jnp.ones((r, r, 1, c), dtype=x.dtype)
            return lax.conv_general_dilated(x, kernel, window_strides=(1, 1), padding='SAME', dimension_numbers=('NHWC', 'HWIO', 'NHWC'), feature_group_count=c)
        key = jax.random.key(seed)
        B, H, W, C = (16, 224, 224, 32)
        x = jax.random.normal(key, (B, H, W, C), dtype=jnp.float32)
        return {'x': x, 'gamma': jnp.ones((C,), jnp.float32), 'beta': jnp.zeros((C,), jnp.float32), 'moving_mean': jnp.zeros((C,), jnp.float32), 'moving_var': jnp.ones((C,), jnp.float32)}
    _L0_conv_all = _L0_conv_setup()
    _L0_conv_in = {k: v for k, v in _L0_conv_all.items() if k in ('gamma', 'beta', 'moving_mean', 'moving_var', )}
    del _L0_conv_all

    def _L1_conv_setup():
        import jax, jax.numpy as jnp
        import numpy as np
        KX = 32
        KY = 32

        def dct_matrix(N):
            n = jnp.arange(N, dtype=jnp.float32)
            k = n[:, None]
            D = jnp.cos(jnp.pi * (n[None, :] + 0.5) * k / N)
            scale = jnp.where(jnp.arange(N) == 0, jnp.sqrt(1.0 / N), jnp.sqrt(2.0 / N))
            return (D * scale[:, None]).astype(jnp.float32)
        key = jax.random.key(seed)
        ks = jax.random.split(key, 5)
        B, nX, nY, dv = (16, 256, 256, 32)
        x = jax.random.normal(ks[0], (B, nX, nY, dv), dtype=jnp.float32)
        R_real = jax.random.uniform(ks[1], (KX, KY, dv, dv), dtype=jnp.float32)
        R_imag = jax.random.uniform(ks[2], (KX, KY, dv, dv), dtype=jnp.float32)
        W = jax.random.normal(ks[3], (dv, dv), dtype=jnp.float32) * (1.0 / np.sqrt(dv))
        b = jax.random.normal(ks[4], (dv,), dtype=jnp.float32) * 0.05
        return {'x': x, 'R_real': R_real, 'R_imag': R_imag, 'W': W, 'b': b}
    _L1_conv_all = _L1_conv_setup()
    _L1_conv_in = {k: v for k, v in _L1_conv_all.items() if k in ('R_real', 'R_imag', 'W', 'b', )}
    del _L1_conv_all

    def _L2_conv_setup():
        import jax, jax.numpy as jnp
        import numpy as np
        from jax import lax
        LENGTH = 7
        SIGMA = 1.5
        CHANNELS = 32

        def gaussian_kernel(length, sigma):
            axis = jnp.linspace(-(length - 1) / 2.0, (length - 1) / 2.0, length)
            g = jnp.exp(-0.5 * axis ** 2 / sigma ** 2)
            k = jnp.outer(g, g)
            return (k / jnp.sum(k)).astype(jnp.float32)
        key = jax.random.key(seed)
        kx, = jax.random.split(key, 1)
        x = jax.random.normal(kx, (8, 512, 512, CHANNELS), dtype=jnp.float32)
        k2d = gaussian_kernel(LENGTH, SIGMA)
        W = jnp.broadcast_to(k2d[:, :, None, None], (LENGTH, LENGTH, 1, CHANNELS)).astype(jnp.float32)
        b = jnp.zeros((CHANNELS,), dtype=jnp.float32)
        return {'x': x, 'W': W, 'b': b}
    _L2_conv_all = _L2_conv_setup()
    _L2_conv_in = {k: v for k, v in _L2_conv_all.items() if k in ('W', 'b', )}
    del _L2_conv_all

    def _L3_conv_setup():
        import jax, jax.numpy as jnp
        import jax.scipy.fft as jsp_fft
        import numpy as np
        B, NX, NY, DV = (4, 512, 512, 32)
        KX, KY = (64, 64)
        key = jax.random.key(seed)
        k1, k2, k3 = jax.random.split(key, 3)
        x = jax.random.normal(k1, (B, NX, NY, DV), dtype=jnp.float32)
        R_real = jax.random.uniform(k2, (DV, DV, KX, KY), dtype=jnp.float32)
        R_imag = jax.random.uniform(k3, (DV, DV, KX, KY), dtype=jnp.float32)
        return {'x': x, 'R_real': R_real, 'R_imag': R_imag}
    _L3_conv_all = _L3_conv_setup()
    _L3_conv_in = {k: v for k, v in _L3_conv_all.items() if k in ('R_real', 'R_imag', )}
    del _L3_conv_all

    return {
        "x": x,
        "L0_conv_gamma": _L0_conv_in["gamma"],
        "L0_conv_beta": _L0_conv_in["beta"],
        "L0_conv_moving_mean": _L0_conv_in["moving_mean"],
        "L0_conv_moving_var": _L0_conv_in["moving_var"],
        "L1_conv_R_real": _L1_conv_in["R_real"],
        "L1_conv_R_imag": _L1_conv_in["R_imag"],
        "L1_conv_W": _L1_conv_in["W"],
        "L1_conv_b": _L1_conv_in["b"],
        "L2_conv_W": _L2_conv_in["W"],
        "L2_conv_b": _L2_conv_in["b"],
        "L3_conv_R_real": _L3_conv_in["R_real"],
        "L3_conv_R_imag": _L3_conv_in["R_imag"],
    }

def reference(x, L0_conv_gamma, L0_conv_beta, L0_conv_moving_mean, L0_conv_moving_var, L1_conv_R_real, L1_conv_R_imag, L1_conv_W, L1_conv_b, L2_conv_W, L2_conv_b, L3_conv_R_real, L3_conv_R_imag):
    import jax
    import jax.numpy as jnp
    def _L0_conv_ref(x, gamma, beta, moving_mean, moving_var):
        import jax, jax.numpy as jnp
        import numpy as np
        from jax import lax
        MAX_SCALE = 4
        SCALES = [2 ** i for i in range(1, MAX_SCALE + 1)]
        EPS_K = 1e-07
        BN_EPS = 0.001

        def sample_min_max_scaling(x):
            mn = jnp.min(x, axis=(1, 2, 3), keepdims=True)
            mx = jnp.max(x, axis=(1, 2, 3), keepdims=True)
            return (x - mn) / (mx - mn + EPS_K)

        def box_sum(x, r):
            c = x.shape[-1]
            kernel = jnp.ones((r, r, 1, c), dtype=x.dtype)
            return lax.conv_general_dilated(x, kernel, window_strides=(1, 1), padding='SAME', dimension_numbers=('NHWC', 'HWIO', 'NHWC'), feature_group_count=c)
        x = sample_min_max_scaling(x)
        measures = jnp.stack([box_sum(x, r) for r in SCALES], axis=-1)
        log_scales = jnp.log(jnp.asarray(SCALES, dtype=x.dtype))
        log_measures = jnp.log(measures + EPS_K)
        mean_ls = jnp.mean(log_scales)
        mean_lm = jnp.mean(log_measures, axis=-1, keepdims=True)
        dls = log_scales - mean_ls
        num = jnp.sum((log_measures - mean_lm) * dls, axis=-1)
        den = jnp.sum(dls ** 2)
        alphas = num / den
        return (alphas - moving_mean) / jnp.sqrt(moving_var + BN_EPS) * gamma + beta

    def _L1_conv_ref(x, R_real, R_imag, W, b):
        import jax, jax.numpy as jnp
        import numpy as np
        KX = 32
        KY = 32

        def dct_matrix(N):
            n = jnp.arange(N, dtype=jnp.float32)
            k = n[:, None]
            D = jnp.cos(jnp.pi * (n[None, :] + 0.5) * k / N)
            scale = jnp.where(jnp.arange(N) == 0, jnp.sqrt(1.0 / N), jnp.sqrt(2.0 / N))
            return (D * scale[:, None]).astype(jnp.float32)
        B, nX, nY, dv = x.shape
        R = R_real + 1j * R_imag
        D = dct_matrix(nY)
        v = jnp.moveaxis(x, -1, -3)
        v = jnp.einsum('kn,bcxn->bcxk', D, v)
        v = jnp.fft.rfft(v, axis=-2, norm='ortho')
        vt = v[..., :KX, :KY]
        vt = jnp.einsum('ijab,ejab->eiab', R, vt)
        nXf = nX // 2 + 1
        spec = jnp.zeros((B, dv, nXf, nY), dtype=vt.dtype).at[..., :KX, :KY].set(vt)
        u = jnp.fft.irfft(spec, n=nX, axis=-2, norm='ortho')
        u = jnp.einsum('kn,bcxk->bcxn', D, u)
        v_out = jnp.moveaxis(u, -3, -1)
        w = x @ W.T + b
        return jax.nn.relu(v_out + w)

    def _L2_conv_ref(x, W, b):
        import jax, jax.numpy as jnp
        import numpy as np
        from jax import lax
        LENGTH = 7
        SIGMA = 1.5
        CHANNELS = 32

        def gaussian_kernel(length, sigma):
            axis = jnp.linspace(-(length - 1) / 2.0, (length - 1) / 2.0, length)
            g = jnp.exp(-0.5 * axis ** 2 / sigma ** 2)
            k = jnp.outer(g, g)
            return (k / jnp.sum(k)).astype(jnp.float32)
        C = x.shape[-1]
        y = lax.conv_general_dilated(x, W, window_strides=(1, 1), padding='SAME', dimension_numbers=('NHWC', 'HWIO', 'NHWC'), feature_group_count=C)
        return jax.nn.relu(y + b) * SIGMA ** 2

    def _L3_conv_ref(x, R_real, R_imag):
        import jax, jax.numpy as jnp
        import jax.scipy.fft as jsp_fft
        import numpy as np
        B, NX, NY, DV = (4, 512, 512, 32)
        KX, KY = (64, 64)
        R = R_real + 1j * R_imag
        kX, kY = R.shape[-2:]
        nX = x.shape[1]
        xt = jnp.moveaxis(x, -1, -3)
        xd = jsp_fft.dct(xt, type=2, axis=-1, norm='ortho')
        xf = jnp.fft.rfft(xd, axis=-2, norm='ortho')
        nXf, nY = xf.shape[-2:]
        xtr = xf[..., :kX, :kY]
        y = jnp.einsum('ijab,ejab->eiab', R, xtr)
        yp = jnp.pad(y, ((0, 0), (0, 0), (0, nXf - kX), (0, nY - kY)))
        yr = jnp.fft.irfft(yp, n=nX, axis=-2, norm='ortho')
        yd = jsp_fft.idct(yr, type=2, axis=-1, norm='ortho')
        return jnp.moveaxis(yd, -3, -1)

    def _gn(v, G=16, eps=1e-5):
        B_, H_, W_, C_ = v.shape
        g = v.reshape(B_, H_, W_, G, C_ // G)
        m = jnp.mean(g, axis=(1, 2, 4), keepdims=True)
        s = jnp.var(g, axis=(1, 2, 4), keepdims=True)
        return ((g - m) / jnp.sqrt(s + eps)).reshape(v.shape)

    def _ln_c(v, eps=1e-6):
        m = jnp.mean(v, axis=-1, keepdims=True)
        s = jnp.var(v, axis=-1, keepdims=True)
        return (v - m) / jnp.sqrt(s + eps)

    def _ln_t(v, eps=1e-5):
        m = jnp.mean(v, axis=-1, keepdims=True)
        s = jnp.var(v, axis=-1, keepdims=True)
        return (v - m) / jnp.sqrt(s + eps)

    def _to_tokens(v):
        B_, H_, W_, C_ = v.shape
        return v.reshape(B_, H_ * W_, C_)
    def _from_tokens(t, like):
        return t.reshape(like.shape)

    x = x + _L0_conv_ref(_gn(x), L0_conv_gamma, L0_conv_beta, L0_conv_moving_mean, L0_conv_moving_var)
    x = x + _L1_conv_ref(_gn(x), L1_conv_R_real, L1_conv_R_imag, L1_conv_W, L1_conv_b)
    x = x + _L2_conv_ref(_gn(x), L2_conv_W, L2_conv_b)
    x = x + _L3_conv_ref(_gn(x), L3_conv_R_real, L3_conv_R_imag)
    return x


_drawn_inputs = setup_inputs


def setup_inputs(seed=0):
    import zlib

    import numpy as np

    out = dict(_drawn_inputs(seed))
    spreads = {'L0_conv_gamma': (1.0, 0.2),
     'L0_conv_beta': (0.0, 0.316),
     'L0_conv_moving_mean': (0.0, 0.313),
     'L0_conv_moving_var': (1.0, 0.2),
     'L2_conv_b': (0.0, 0.425)}
    factors = {'L1_conv_b': 8.0}
    for name, (base, spread) in spreads.items():
        noise = np.random.default_rng([zlib.crc32(name.encode()), seed]).standard_normal(out[name].shape)
        drawn = base * np.exp(spread * noise) if base else spread * noise
        out[name] = jnp.asarray(drawn.astype(out[name].dtype))
    for name, factor in factors.items():
        out[name] = (out[name] * factor).astype(out[name].dtype)
    return out
```

```python
import numpy as np
import concourse.bass as bass
from concourse import mybir
from contextlib import ExitStack

F32 = mybir.dt.float32
ALU = mybir.AluOpType
ACT = mybir.ActivationFunctionType
AX = mybir.AxisListType

H = 224
W = 224
C = 32
G = 16
T = 2
P = 128
ROW0 = (0, H - P)
ONCE = (slice(0, H // 2), slice(P - H // 2, P))
HALF = W // 2
CG = 4
NCG = C // CG
GN_EPS = 1e-5
ROWSTAT = 1.0 / (2 * H)
PAD = 8
WP = 240
SCALES = (16, 8, 2, 4)
LEVEL = {2: 1, 4: 2, 8: 3, 16: 0}


class Steps:

    def __init__(self, engine, sem):
        self.engine, self.sem, self.base, self.k = engine, sem, 0, 0

    def done(self, instruction):
        instruction.then_inc(self.sem, 1)
        self.k += 1

    def settle(self):
        self.engine.wait_ge(self.sem, self.base + self.k)

    def enter(self, i, per_turn):
        self.start, self.per_turn = self.base + self.k, per_turn
        self.base, self.k = i * per_turn + self.start, 0

    def leave(self, turns):
        assert self.k == self.per_turn, (self.k, self.per_turn)
        self.base, self.k = self.start + self.per_turn * turns, 0


def after(engine, sem, count):
    if not isinstance(count, int) or count > 0:
        engine.wait_ge(sem, count)


class Sample:

    def __init__(self, i, off):
        self.e, self.par, self.use = i * 2 + off, off % 2, i + off // 2


class GroupStats:

    def __init__(self, sb, name, segments, count, ahead=False):
        self.segments, self.count = segments, count
        self.bn = sb(name + "_bn", [P, segments, G, 6])
        self.rows = sb(name + "_rows", [P, segments, G, 6]) if ahead else self.bn
        self.gm = sb(name + "_gm", [P, G])
        self.dev = sb(name + "_dev", [P, segments, G, 2])
        self.var = sb(name + "_var", [P, G])
        self.rs = sb(name + "_rs", [P, G])
        self.t1 = sb(name + "_t1", [P, G])
        self.t2 = sb(name + "_t2", [P, G])
        self.ab = sb(name + "_ab", [P, 2, G, 2])

    def hand_over(self, dve, steps, last, sem):
        steps.done(last)
        steps.settle()
        dve.tensor_copy(self.bn[:].rearrange("p s g v -> p (s g v)"),
                        self.rows[:].rearrange("p s g v -> p (s g v)")).then_inc(sem, 1)

    def pe_mean(self, pe, st, once, tile_of, sem):
        for s in range(self.segments):
            last = pe.matmul(st[:, 0:C], once[:, tile_of(s), :], self.bn[:, s, :, 1:6:3],
                             start=(s == 0), stop=(s == self.segments - 1))
        last.then_inc(sem, 1)

    def dve_deviations(self, dve, steps, st, sem):
        steps.done(dve.tensor_reduce(self.gm[:], st[:, 0:C].rearrange("p (g k) -> p g k", k=2),
                                     axis=AX.X, op=ALU.add))
        steps.settle()
        for s in range(self.segments):
            last = dve.tensor_tensor(self.dev[:, s], self.bn[:, s, :, 1:6:3],
                                     self.gm[:].unsqueeze(2).to_broadcast([P, G, 2]), ALU.subtract)
        steps.done(last)
        steps.settle()
        flat = self.dev[:].rearrange("p s g k -> p (s g k)")
        steps.done(dve.tensor_tensor(flat, flat, flat, ALU.mult))
        steps.settle()
        pairs = self.dev[:].rearrange("p s g k -> p (s g) k")
        dve.scalar_tensor_tensor(out=pairs, in0=self.bn[:].rearrange("p s g v -> p (s g) v")[:, :, 2:6:3],
                                 scalar=1.0 / self.count, in1=pairs, op0=ALU.mult,
                                 op1=ALU.add).then_inc(sem, 1)

    def pe_variance(self, pe, st, once, tile_of, sem):
        for s in range(self.segments):
            last = pe.matmul(st[:, C:2 * C], once[:, tile_of(s), :], self.dev[:, s],
                             start=(s == 0), stop=(s == self.segments - 1))
        last.then_inc(sem, 1)

    def dve_variance(self, dve, steps, st, sem):
        steps.done(dve.tensor_reduce(self.t1[:], st[:, C:2 * C].rearrange("p (g k) -> p g k", k=2),
                                     axis=AX.X, op=ALU.add))
        steps.settle()
        dve.tensor_scalar(self.var[:], self.t1[:], GN_EPS, None, ALU.add).then_inc(sem, 1)

    def dve_scales(self, dve, steps):
        newton(dve, steps, self.var[:], self.rs[:], self.t1[:], self.t2[:])
        steps.done(dve.scalar_tensor_tensor(out=self.t2[:], in0=self.gm[:], scalar=-1.0, in1=self.rs[:],
                                            op0=ALU.mult, op1=ALU.mult))
        steps.settle()
        dve.tensor_copy(self.ab[:, 0], self.rs[:].unsqueeze(2).to_broadcast([P, G, 2]))
        steps.done(dve.tensor_copy(self.ab[:, 1], self.t2[:].unsqueeze(2).to_broadcast([P, G, 2])))
        steps.settle()

    def row(self, k):
        return self.ab[:, k].rearrange("p g k -> p (g k)")


def newton(dve, steps, v, y, t1, t2):
    steps.done(dve.tensor_tensor(t1, y, y, ALU.mult))
    steps.settle()
    steps.done(dve.scalar_tensor_tensor(out=t2, in0=t1, scalar=-0.5, in1=v, op0=ALU.mult, op1=ALU.mult))
    steps.settle()
    steps.done(dve.tensor_scalar(t1, t2, 1.5, None, ALU.add))
    steps.settle()
    steps.done(dve.tensor_tensor(y, y, t1, ALU.mult))
    steps.settle()


def on_columns(pe, st, rows4, one, sem):
    for k in range(2):
        last = pe.matmul(st[:, 64 + k:65 + k], rows4[0:1, k, :], one[0:1, 0:1], start=True, stop=True)
    last.then_inc(sem, 1)


class Scope(ExitStack):

    def __init__(self, nc, prefix):
        super().__init__()
        self.nc, self.prefix = nc, prefix

    def sb(self, name, shape, dtype=F32):
        return self.enter_context(self.nc.sbuf_tensor(self.prefix + name, shape, dtype))

    def ps(self, name, shape):
        return self.enter_context(self.nc.psum_tensor(self.prefix + name, shape, F32))

    def sem(self, name):
        return self.enter_context(self.nc.semaphore(self.prefix + name))


def pass_fractal(nc, B, d, keep):
    UN = NCG * T
    with Scope(nc, "a_") as z:
        X = z.sb("X", [P, 2, T, W, C])
        Hb = z.sb("H", [P, 2, 4, CG, WP])
        L = z.sb("L", [P, 2, len(SCALES), CG, W])
        Zs = z.sb("Zs", [HALF, 2, 64 * C])
        SO = z.sb("SO", [P, 512])
        band = z.sb("band", [P, 4, P])
        Fr = z.sb("F", [P, T, 64])
        Dc = z.sb("D", [HALF, 2, 32])
        once = z.sb("once", [P, T, P])
        ident = z.sb("ident", [P, P])
        ones2 = z.sb("ones2", [2, P])
        half = z.sb("half", [P, C])
        eps = z.sb("eps", [P, 1])
        par4 = z.sb("par4", [P, 4, C])
        alp = z.sb("alp", [P, 2, C])
        mv = z.sb("mv", [P, 4, C])
        MM = z.sb("MM", [P, T, 2, C])
        mx = z.sb("mx", [P, 2, C])
        nm = z.sb("nm", [P, 2])
        ext = z.sb("ext", [2, 3])
        rng = z.sb("rng", [P, 4])
        credit = z.sb("credit", [1, 2])
        cf = z.sb("cf", [P, 2, 2, C])
        rows4 = z.sb("rows4", [1, 2, P])
        sx = GroupStats(z.sb, "sx", T, W)
        s1 = GroupStats(z.sb, "s1", T, W, ahead=True)
        PS = z.ps("PS", [P, 8, 512])
        STX, ST1 = PS[:, 7, 256:512], PS[:, 7, 0:256]

        names = ("const_in", "x_in0", "x_in1", "xs_ready", "h_ready", "m_ready", "ln_done", "t_ready",
                 "z_ready", "x1_ready", "zps_ready", "zev_done", "modes_ready", "modes_out", "modes_stored",
                 "x1_stored", "coef_ready", "sx_in", "sx_out", "s1_in", "s1_out", "root_in", "root_out",
                 "dve_step", "setup")
        sem = {n: z.sem(n) for n in names}
        x_in = (sem["x_in0"], sem["x_in1"])
        block = z.enter_context(nc.Block())

        def U(s, u):
            return s.e * UN + u

        def turns(body):
            body(None, None, Sample(0, 0))
            body(None, Sample(0, 0), Sample(0, 1))
            return (B - 2) // 2

        def looped(engine, body, steps=None, per_turn=0):
            n = turns(body)
            with engine.Fori(0, n) as i:
                if steps:
                    steps.enter(i, per_turn)
                body(Sample(i, 0), Sample(i, 1), Sample(i, 2))
                body(Sample(i, 1), Sample(i, 2), Sample(i, 3))
            if steps:
                steps.leave(n)
            body(Sample(n, 0), Sample(n, 1), None)
            body(Sample(n, 1), None, None)

        @block.sync
        def _(sp):
            for dst, src in ((band, d["band"]), (Fr, d["F1"]), (Dc, d["D1"]), (once, d["once1"]),
                             (ident, d["ident"])):
                sp.dma_start(dst[:], src).then_inc(sem["const_in"], 16)
            for k, name in enumerate(("gamma", "beta", "mean", "var")):
                sp.dma_start(par4[:, k, :], d[name].rearrange("(a c) -> a c", a=1).to_broadcast([P, C]))\
                  .then_inc(sem["const_in"], 16)

            def load(s):
                for t in range(T):
                    sp.dma_start(X[:, s.par, t], d["x"][s.e, ROW0[t]:ROW0[t] + P]).then_inc(x_in[s.par], 16)

            def finish(s, following):
                after(sp, sem["x1_ready"], U(s, UN))
                for t in range(T):
                    r0 = t * (H // 2)
                    sp.dma_start(d["x1"][s.e, r0:r0 + H // 2], X[ONCE[t], s.par, t])\
                      .then_inc(sem["x1_stored"], 16)
                if following is not None:
                    after(sp, sem["x1_stored"], s.e * 32 + 32)
                    after(sp, sem["s1_in"], s.e * 3 + 1)
                    after(sp, sem["zps_ready"], s.e * NCG + NCG)
                    load(following)
                after(sp, sem["modes_out"], s.e + 2)
                sp.dma_start(d["spec1"][s.e], SO[:]).then_inc(sem["modes_stored"], 16)

            load(Sample(0, 0))
            load(Sample(0, 1))
            n = (B - 2) // 2
            with sp.Fori(0, n) as i:
                finish(Sample(i, 0), Sample(i, 2))
                finish(Sample(i, 1), Sample(i, 3))
            finish(Sample(n, 0), None)
            finish(Sample(n, 1), None)
            sp.wait_ge(sem["x1_stored"], B * 32)
            sp.wait_ge(sem["modes_stored"], B * 16 + 16)

        @block.gpsimd
        def _(pool):
            pool.memset(ones2[:], 1.0)
            pool.memset(eps[:], 1e-7)
            pool.memset(Hb[:], 0.0)
            pool.memset(half[:], -0.5).then_inc(sem["setup"], 1)
            pool.memset(credit[:, 0:1], 0.0).then_inc(sem["modes_out"], 1)
            pool.memset(credit[:, 1:2], 0.0).then_inc(sem["modes_stored"], 16)

            def root(stats, k):
                pool.wait_ge(sem["root_in"], k)
                pool.tensor_tensor(stats.rs[:], stats.var[:], half[:, 0:G], ALU.pow).then_inc(sem["root_out"], 1)

            pool.wait_ge(sem["setup"], 1)
            pool.wait_ge(sem["root_in"], 1)
            pool.tensor_tensor(mv[:, 1], mv[:, 0], half[:], ALU.pow).then_inc(sem["root_out"], 1)
            root(sx, 2)
            root(sx, 3)
            with pool.Fori(0, B - 2) as i:
                root(s1, i * 2 + 4)
                root(sx, i * 2 + 5)
            root(s1, 2 * B)
            root(s1, 2 * B + 1)

        def root_count(s, of_x):
            if of_x:
                return s.e * 2 + 1 if not isinstance(s.e, int) or s.e >= 1 else 2
            return s.e * 2 + 4 if not isinstance(s.e, int) or s.e < B - 1 else 2 * B + 1

        @block.scalar
        def _(act):
            def scale(s, u):
                cg, t = divmod(u, T)
                if u == 0:
                    after(act, sem["coef_ready"], s.e + 1)
                    after(act, x_in[s.par], s.use * 32 + 32)
                after(act, sem["m_ready"], U(s, u) * 4 - 4)
                for k in range(CG):
                    c = cg * CG + k
                    last = act.activation(Hb[:, u % 2, 0, k, PAD:PAD + W], X[:, s.par, t, :, c], ACT.Relu,
                                          scale=cf[:, s.par, 0, c:c + 1], bias=cf[:, s.par, 1, c:c + 1])
                last.then_inc(sem["xs_ready"], 1)

            def logs(s, u):
                after(act, sem["x1_ready"], U(s, u) - 1)
                for j in range(4):
                    ch, sp_ = divmod(j, 2)
                    after(act, sem["m_ready"], U(s, u) * 4 + (j + 1))
                    out = L[:, u % 2, 2 * sp_:2 * sp_ + 2, 2 * ch:2 * ch + 2, :].rearrange("p s c y -> p s (c y)")
                    b0 = 2 * (j % 2)
                    act.activation(out, PS[:, b0:b0 + 2, 0:2 * W], ACT.Ln, bias=eps[:, 0:1])\
                       .then_inc(sem["ln_done"], 1)

            def affine(s, u):
                cg = u // T
                after(act, sem["t_ready"], U(s, u) + 1)
                for k in range(CG):
                    c = cg * CG + k
                    last = act.activation(L[:, u % 2, 2, k], L[:, u % 2, 0, k], ACT.Identity,
                                          scale=alp[:, 0, c:c + 1], bias=alp[:, 1, c:c + 1])
                last.then_inc(sem["z_ready"], 1)

            def keep_rows_done(s, cg):
                if cg == 0:
                    after(act, sem["modes_ready"], s.e)
                after(act, sem["zps_ready"], s.e * NCG + (cg + 1))
                for yc in range(2):
                    last = act.activation(
                        Zs[:, yc].rearrange("p (q c) -> p c q", c=C)[:, CG * cg:CG * cg + CG, :],
                        PS[0:HALF, 4 + cg % 2].rearrange("p (c y q) -> p c y q", c=CG, y=2)[:, :, yc],
                        ACT.Copy)
                last.then_inc(sem["zev_done"], 1)

            def body(prev, cur, nxt):
                for u in range(UN):
                    if u < UN - 1:
                        if cur:
                            scale(cur, u + 1)
                    elif nxt:
                        scale(nxt, 0)
                    if prev and u == 0:
                        keep_rows_done(prev, 6)
                    if prev and u == 2:
                        keep_rows_done(prev, 7)
                    if prev and u == 4:
                        after(act, sem["modes_ready"], prev.e + 1)
                        after(act, sem["modes_stored"], prev.e * 16 + 16)
                        act.activation(SO[:], PS[:, 6, :], ACT.Copy).then_inc(sem["modes_out"], 1)
                    if cur and u >= 4 and u % 2 == 0:
                        keep_rows_done(cur, u // 2 - 2)
                    if cur:
                        logs(cur, u)
                    if u > 0 and cur:
                        affine(cur, u - 1)
                    if u == 0 and prev:
                        affine(prev, UN - 1)

            act.wait_ge(sem["setup"], 2)
            looped(act, body)

        @block.tensor
        def _(pe):
            def boxes(s, u):
                after(pe, sem["h_ready"], U(s, u) + 1)
                for j in range(4):
                    ch, sp_ = divmod(j, 2)
                    after(pe, sem["ln_done"], U(s, u) * 4 + (j - 1))
                    for k in range(2):
                        pos = 2 * sp_ + k
                        last = pe.matmul(PS[:, 2 * (j % 2) + k, 0:2 * W], band[:, pos, :],
                                         Hb[:, u % 2, LEVEL[SCALES[pos]], 2 * ch:2 * ch + 2, PAD:PAD + W],
                                         start=True, stop=True)
                    last.then_inc(sem["m_ready"], 1)

            def over_rows(s, cg):
                after(pe, sem["x1_ready"], U(s, 2 * cg + 2))
                after(pe, sem["zev_done"], s.e * NCG + (cg - 1))
                for k in range(CG):
                    for yc in range(2):
                        q0 = (k * 2 + yc) * 64
                        for t in range(T):
                            last = pe.matmul(PS[0:HALF, 4 + cg % 2, q0:q0 + 64],
                                             X[:, s.par, t, yc * HALF:(yc + 1) * HALF, cg * CG + k],
                                             Fr[:, t, :], start=(t == 0), stop=(t == T - 1))
                last.then_inc(sem["zps_ready"], 1)

            def over_columns(s):
                after(pe, sem["zev_done"], s.e * NCG + NCG)
                after(pe, sem["modes_out"], s.e + 1)
                for ap in range(16):
                    for yc in range(2):
                        last = pe.matmul(PS[:, 6, ap * 32:ap * 32 + 32], Zs[:, yc, ap * P:ap * P + P],
                                         Dc[:, yc, :], start=(yc == 0), stop=(yc == 1))
                last.then_inc(sem["modes_ready"], 1)

            def body(prev, cur, nxt):
                for u in range(UN):
                    if prev and u == 3:
                        after(pe, sem["s1_in"], prev.e * 3 + 1)
                        s1.pe_mean(pe, ST1, once, lambda s: s, sem["s1_out"])
                        over_columns(prev)
                    if prev and u == 4:
                        after(pe, sem["s1_in"], prev.e * 3 + 2)
                        s1.pe_variance(pe, ST1, once, lambda s: s, sem["s1_out"])
                    if prev and u == 6:
                        after(pe, sem["s1_in"], prev.e * 3 + 3)
                        on_columns(pe, ST1, rows4, ones2, sem["s1_out"])
                    if nxt and u == 11:
                        after(pe, sem["sx_in"], nxt.e * 4 + 1)
                        sx.pe_mean(pe, STX, once, lambda s: s, sem["sx_out"])
                    if nxt and u == 12:
                        after(pe, sem["sx_in"], nxt.e * 4 + 2)
                        sx.pe_variance(pe, STX, once, lambda s: s, sem["sx_out"])
                    if nxt and u == 14:
                        after(pe, sem["sx_in"], nxt.e * 4 + 3)
                        pe.matmul(STX[0:2, 64:64 + P], nm[:], ident[:], start=True, stop=True)\
                          .then_inc(sem["sx_out"], 1)
                    if nxt and u == 15:
                        after(pe, sem["sx_in"], nxt.e * 4 + 4)
                        pe.matmul(STX[:, 192:194], ones2[:], ext[:, 1:3], start=True, stop=True)\
                          .then_inc(sem["sx_out"], 1)
                    if cur:
                        boxes(cur, u)
                    if prev and u == 1:
                        over_rows(prev, 7)
                    if cur and u >= 3 and u % 2 == 1:
                        over_rows(cur, (u - 3) // 2)

            pe.wait_ge(sem["const_in"], 9 * 16)
            pe.wait_ge(sem["setup"], 1)
            looped(pe, body)

        @block.vector
        def _(dve):
            steps = Steps(dve, sem["dve_step"])
            dve.wait_ge(sem["const_in"], 9 * 16)
            dve.wait_ge(sem["setup"], 1)
            dve.tensor_scalar(mv[:, 0], par4[:, 3], 0.001, None, ALU.add).then_inc(sem["root_in"], 1)
            dve.wait_ge(sem["root_in"], 1)
            dve.wait_ge(sem["root_out"], 1)
            newton(dve, steps, mv[:, 0], mv[:, 1], mv[:, 2], mv[:, 3])
            steps.done(dve.tensor_tensor(mv[:, 2], mv[:, 1], par4[:, 0], ALU.mult))
            steps.settle()
            steps.done(dve.tensor_tensor(mv[:, 3], mv[:, 2], par4[:, 2], ALU.mult))
            steps.settle()
            steps.done(dve.tensor_scalar(alp[:, 0], mv[:, 2], float(0.1 / np.log(2.0)), None, ALU.mult))
            steps.done(dve.tensor_tensor(alp[:, 1], par4[:, 1], mv[:, 3], ALU.subtract))
            steps.settle()
            dve.tensor_copy(mv[:, 0], mv[:, 1]).then_inc(sem["setup"], 1)

            def sums(s, u):
                after(dve, sem["xs_ready"], U(s, u) + 1)
                after(dve, sem["m_ready"], U(s, u) * 4 - 4)
                h = Hb[:, u % 2]
                steps.done(dve.tensor_tensor(h[:, 1, :, 1:239], h[:, 0, :, 1:239], h[:, 0, :, 2:240], ALU.add))
                steps.settle()
                steps.done(dve.tensor_tensor(h[:, 2, :, 2:238], h[:, 1, :, 1:237], h[:, 1, :, 3:239], ALU.add))
                steps.settle()
                steps.done(dve.tensor_tensor(h[:, 3, :, 4:236], h[:, 2, :, 2:234], h[:, 2, :, 6:238], ALU.add))
                steps.settle()
                dve.tensor_tensor(h[:, 0, :, 8:232], h[:, 3, :, 4:228], h[:, 3, :, 12:236], ALU.add)\
                   .then_inc(sem["h_ready"], 1)

            def combine(s, u):
                after(dve, sem["ln_done"], U(s, u) * 4 + 4)
                lu = L[:, u % 2].rearrange("p s c y -> p s (c y)")
                steps.done(dve.tensor_tensor(lu[:, 0:2], lu[:, 0:2], lu[:, 2:4], ALU.subtract))
                steps.settle()
                dve.scalar_tensor_tensor(out=lu[:, 0], in0=lu[:, 0], scalar=3.0, in1=lu[:, 1],
                                         op0=ALU.mult, op1=ALU.add).then_inc(sem["t_ready"], 1)

            def add(s, u):
                cg, t = divmod(u, T)
                after(dve, sem["z_ready"], U(s, u) + 1)
                xv = X[:, s.par, t, :, cg * CG:cg * CG + CG].rearrange("p y c -> p c y")
                dve.tensor_tensor(xv, xv, L[:, u % 2, 2], ALU.add).then_inc(sem["x1_ready"], 1)

            def stats_of_x1(s, u):
                cg, t = divmod(u, T)
                after(dve, sem["x1_ready"], U(s, u) + 1)
                for g in (2 * cg, 2 * cg + 1):
                    last = dve.bn_stats(s1.rows[:, t, g, :], X[:, s.par, t, :, 2 * g:2 * g + 2])
                if u == UN - 1:
                    s1.hand_over(dve, steps, last, sem["s1_in"])

            def stats_of_x(s, k):
                t, cg = divmod(k, NCG)
                if k == 0:
                    after(dve, x_in[s.par], s.use * 32 + 32)
                for g in (2 * cg, 2 * cg + 1):
                    dve.bn_stats(sx.bn[:, t, g, :], X[:, s.par, t, :, 2 * g:2 * g + 2])
                xv = X[:, s.par, t, :, cg * CG:cg * CG + CG].rearrange("p y c -> p c y")
                dve.tensor_reduce(MM[:, t, 0, cg * CG:cg * CG + CG], xv, axis=AX.X, op=ALU.max)
                last = dve.tensor_reduce(MM[:, t, 1, cg * CG:cg * CG + CG], xv, axis=AX.X, op=ALU.min)
                if k == 2 * NCG - 1:
                    last.then_inc(sem["sx_in"], 1)

            def extremes(s):
                steps.done(dve.tensor_tensor(mx[:, 0], MM[:, 0, 0], MM[:, 1, 0], ALU.max))
                steps.done(dve.tensor_tensor(mx[:, 1], MM[:, 0, 1], MM[:, 1, 1], ALU.min))
                steps.settle()
                steps.done(dve.tensor_tensor(mx[:, 0], mx[:, 0], sx.row(0), ALU.mult))
                steps.done(dve.scalar_tensor_tensor(out=mx[:, 1], in0=mx[:, 1], scalar=-1.0, in1=sx.row(0),
                                                    op0=ALU.mult, op1=ALU.mult))
                steps.settle()
                steps.done(dve.tensor_tensor(mx[:, 0], mx[:, 0], sx.row(1), ALU.add))
                steps.done(dve.tensor_tensor(mx[:, 1], mx[:, 1], sx.row(1), ALU.subtract))
                steps.settle()
                dve.tensor_reduce(nm[:], mx[:], axis=AX.X, op=ALU.max).then_inc(sem["sx_in"], 1)

            def body(prev, cur, nxt):
                for u in range(UN):
                    if prev and u == 3:
                        after(dve, sem["s1_out"], prev.e * 3 + 1)
                        s1.dve_deviations(dve, steps, ST1, sem["s1_in"])
                    if prev and u == 4:
                        after(dve, sem["s1_out"], prev.e * 3 + 2)
                        s1.dve_variance(dve, steps, ST1, sem["root_in"])
                    if prev and u == 5:
                        after(dve, sem["root_out"], root_count(prev, False))
                        s1.dve_scales(dve, steps)
                        for k in range(2):
                            last = dve.tensor_copy(
                                rows4[0:1, k].rearrange("p (q c) -> p q c", c=C),
                                s1.row(k)[0:1].unsqueeze(1).to_broadcast([1, 4, C]))
                        last.then_inc(sem["s1_in"], 1)
                    if prev and u == 6:
                        after(dve, sem["s1_out"], prev.e * 3 + 3)
                        steps.done(dve.tensor_copy(keep.acol1[:, bass.ds(prev.e, 1)], ST1[:, 64:65]))
                        steps.done(dve.tensor_copy(keep.bcol1[:, bass.ds(prev.e, 1)], ST1[:, 65:66]))
                    if nxt and u == 11:
                        after(dve, sem["sx_out"], nxt.e * 4 + 1)
                        sx.dve_deviations(dve, steps, STX, sem["sx_in"])
                    if nxt and u == 12:
                        after(dve, sem["sx_out"], nxt.e * 4 + 2)
                        sx.dve_variance(dve, steps, STX, sem["root_in"])
                    if nxt and u == 13:
                        after(dve, sem["root_out"], root_count(nxt, True))
                        sx.dve_scales(dve, steps)
                        extremes(nxt)
                    if nxt and u == 14:
                        after(dve, sem["sx_out"], nxt.e * 4 + 3)
                        steps.done(dve.tensor_reduce(ext[:, 0:1], STX[0:2, 64:64 + P], axis=AX.X, op=ALU.max))
                        steps.settle()
                        dve.tensor_scalar(ext[:, 1:3], ident[0:2, 0:2], ext[:, 0:1], None, ALU.mult)\
                           .then_inc(sem["sx_in"], 1)
                    if nxt and u == 15:
                        after(dve, sem["sx_out"], nxt.e * 4 + 4)
                        steps.done(dve.tensor_copy(rng[:, 0:2], STX[:, 192:194]))
                        steps.settle()
                        steps.done(dve.tensor_tensor(rng[:, 2:3], rng[:, 0:1], rng[:, 1:2], ALU.add))
                        steps.settle()
                        steps.done(dve.tensor_scalar(rng[:, 2:3], rng[:, 2:3], 1e-7, None, ALU.add))
                        steps.settle()
                        steps.done(dve.reciprocal(rng[:, 3:4], rng[:, 2:3]))
                        steps.settle()
                        steps.done(dve.tensor_scalar(cf[:, nxt.par, 0], sx.row(0), rng[:, 3:4], None, ALU.mult))
                        steps.settle()
                        dve.tensor_scalar(cf[:, nxt.par, 1], sx.row(1), rng[:, 1:2], rng[:, 3:4], ALU.add,
                                          ALU.mult).then_inc(sem["coef_ready"], 1)
                    if u < UN - 1:
                        if cur:
                            sums(cur, u + 1)
                    elif nxt:
                        sums(nxt, 0)
                    if cur:
                        combine(cur, u)
                    if u > 0 and cur:
                        add(cur, u - 1)
                    if u == 0 and prev:
                        add(prev, UN - 1)
                    if u > 1 and cur:
                        stats_of_x1(cur, u - 2)
                    if u < 2 and prev:
                        stats_of_x1(prev, UN - 2 + u)
                    if nxt and 3 <= u <= 10:
                        stats_of_x(nxt, 2 * (u - 3))
                        stats_of_x(nxt, 2 * (u - 3) + 1)

            looped(dve, body, steps, per_turn=keep.steps_a)


def mix_modes(nc, name, B, pairs, d, spec, out, R, acol, bcol):
    SC = 128
    n = pairs // SC
    with Scope(nc, name) as z:
        Rb = z.sb("R", [P, 2, SC, 64])
        Xb = z.sb("X", [P, 2, B, SC])
        Yb = z.sb("Y", [P, 2, B, SC])
        corr = z.sb("corr", [C, n, B])
        free = z.sb("free", [1, 4])
        idle = z.sb("idle", [P, P], mybir.dt.bfloat16)
        idle_set = z.sem("idle_set")
        PS = z.ps("PS", [P, 8, 512])
        in_ = (z.sem("in0"), z.sem("in1"))
        out_ = (z.sem("out0"), z.sem("out1"))
        ready, mixed, low, high, step = (z.sem(s) for s in ("ready", "mixed", "low", "high", "step"))
        block = z.enter_context(nc.Block())

        @block.sync
        def _(sp):
            def load(sc, par):
                sp.dma_start(Rb[:, par], R[:, bass.ds(sc * SC, SC), :]).then_inc(in_[par], 16)
                sp.dma_start(Xb[:, par], spec.rearrange("e p m -> p e m")[:, :, bass.ds(sc * SC, SC)])\
                  .then_inc(in_[par], 16)

            load(0, 0)
            load(1, 1)
            with sp.Fori(0, n // 2 - 1) as i:
                for par in range(2):
                    sp.wait_ge(mixed, i * 4 + (2 * par + 2))
                    load(i * 2 + (par + 2), par)

        @block.vector
        def _(dve):
            dve.memset(corr[:], 0.0).then_inc(step, 1)
            dve.wait_ge(step, 1)
            dve.tensor_scalar(corr[:, 0, :], bcol[0:C, :], float(W), None, ALU.mult).then_inc(step, 1)
            dve.wait_ge(step, 2)

            def prepare(sc, par, i):
                dve.wait_ge(in_[par], i * 32 + 32)
                for h in range(2):
                    neg = Rb[64 * h + 32:64 * h + 64, par, :, 0:32]
                    dve.tensor_scalar(neg, neg, -1.0, None, ALU.mult)
                dve.tensor_tensor(Xb[:, par], Xb[:, par], acol[:].unsqueeze(2).to_broadcast([P, B, SC]), ALU.mult)\
                   .then_inc(step, 1)
                dve.wait_ge(step, i * 2 + (3 + par))
                dve.tensor_tensor(Xb[0:C, par, :, 0], Xb[0:C, par, :, 0], corr[:, bass.ds(sc, 1), :].squeeze(1), ALU.add)\
                   .then_inc(ready, 1)

            def collect(i, par, k):
                if k == 0:
                    dve.wait_ge(out_[par], i * 16 + 16)
                dve.wait_ge(mixed, i * 4 + (2 * par + k + 1))
                dve.tensor_copy(Yb[64:128, par, :, 64 * k:64 * k + 64].rearrange("p e (k m) -> p k m e", k=2),
                                PS[64:128, 4 * k + 2:4 * k + 4, 0:32 * B].rearrange("p k (m e) -> p k m e", e=B))\
                   .then_inc(high, 1)

            prepare(0, 0, 0)

            def turn(i, more):
                for par in range(2):
                    if par == 0 or more:
                        prepare(i * 2 + (par + 1), 1 - par, i + par)
                    collect(i, par, 0)
                    collect(i, par, 1)

            with dve.Fori(0, n // 2 - 1) as i:
                turn(i, True)
            turn(n // 2 - 1, False)

        @block.gpsimd
        def _(pool):
            pool.memset(idle[:], 0.0).then_inc(idle_set, 1)
            pool.memset(free[:, 0:1], 0.0).then_inc(low, 2)
            pool.memset(free[:, 1:2], 0.0).then_inc(high, 2)
            pool.memset(free[:, 2:3], 0.0).then_inc(out_[0], 16)
            pool.memset(free[:, 3:4], 0.0).then_inc(out_[1], 16)

        @block.tensor
        def _(pe):
            pe.wait_ge(idle_set, 1)
            with pe.Fori(0, n // 2) as i:
                for par in range(2):
                    pe.wait_ge(ready, i * 2 + (par + 1))
                    for k in range(2):
                        pe.wait_ge(low, i * 4 + (2 * par + k + 1))
                        pe.wait_ge(high, i * 4 + (2 * par + k + 1))
                        pe.ldweights(idle[:], tile_position=(0, 0))
                        for m in range(64):
                            for h in range(2):
                                part = slice(64 * h, 64 * h + 64)
                                last = pe.matmul(PS[part, 4 * k + 2 * h + m // 32, (m % 32) * B:(m % 32) * B + B],
                                                 Rb[part, par, 64 * k + m, :], Xb[part, par, :, 64 * k + m],
                                                 start=True, stop=True)
                        last.then_inc(mixed, 1)

        @block.scalar
        def _(act):
            with act.Fori(0, n // 2) as i:
                for par in range(2):
                    act.wait_ge(out_[par], i * 16 + 16)
                    for k in range(2):
                        act.wait_ge(mixed, i * 4 + (2 * par + k + 1))
                        act.activation(Yb[0:64, par, :, 64 * k:64 * k + 64].rearrange("p e (k m) -> p k m e", k=2),
                                       PS[0:64, 4 * k:4 * k + 2, 0:32 * B].rearrange("p k (m e) -> p k m e", e=B),
                                       ACT.Copy).then_inc(low, 1)
                    act.wait_ge(low, i * 4 + (2 * par + 4))
                    act.wait_ge(high, i * 4 + (2 * par + 4))
                    act.dma_start(out.rearrange("e p m -> p e m")[:, :, bass.ds((i * 2 + par) * SC, SC)], Yb[:, par])\
                       .then_inc(out_[par], 16)
            for par in range(2):
                act.wait_ge(out_[par], (n // 2) * 16 + 16)


def pass_spectral(nc, B, d, keep):
    NQ = W // 16
    RING = 7
    with Scope(nc, "c_") as z:
        XC = z.sb("XC", [P, RING, T, 16 * C])
        XO = z.sb("XO", [P, 2, T, C, HALF])
        Ys = z.sb("Ys", [P, 512])
        UT = z.sb("UT", [C, 16, P])
        V = z.sb("V", [64, W, C])
        XT = z.sb("XT", [P, 2, 512])
        Wbd = z.sb("Wbd", [P, P])
        Ws = z.sb("Ws", [P, P])
        WT = z.sb("WT", [C, C])
        bias = z.sb("bias", [C, 1])
        cst = z.sb("cst", [C, B])
        Di = z.sb("Di", [C, W])
        Gr = z.sb("G", [64, T, P])
        once = z.sb("once", [P, T, P])
        ident = z.sb("ident", [P, P])
        half = z.sb("half", [P, G])
        st = GroupStats(z.sb, "st", 2 * T, HALF)
        PS = z.ps("PS", [P, 8, 512])
        ST = PS[:, 6, :]
        names = ("const_in", "setup", "cst_in", "cst_ready", "ys_in", "ys_ready", "w_ready", "tps_ready",
                 "tev_done", "vps_ready", "vev_done", "xt_ready", "xt_done", "f_ready", "f_done",
                 "half_ready", "st_in", "st_out", "root_in", "root_out", "ab_kept", "dve_step", "store0", "store1")
        sem = {n: z.sem(n) for n in names}
        xin = [z.sem(f"xin{k}") for k in range(RING)]
        stored = (sem["store0"], sem["store1"])
        block = z.enter_context(nc.Block())

        def turns(engine, body, steps=None, per_turn=0):
            body(0, None)
            with engine.Fori(1, B) as e:
                if steps:
                    steps.enter(e - 1, per_turn)
                body(e, e - 1)
            if steps:
                steps.leave(B - 1)
            body(None, B - 1)

        @block.sync
        def _(sp):
            for dst, src in ((Wbd, d["wbd"]), (WT, d["wt"]), (bias, d["b1"]), (Di, d["Di1"]), (Gr, d["G1"]),
                             (once, d["once2"]), (ident, d["ident"])):
                sp.dma_start(dst[:], src).then_inc(sem["const_in"], 16)

            def load(e, q):
                for t in range(T):
                    sp.dma_start(XC[:, q % RING, t],
                                 d["x1"][e, ROW0[t]:ROW0[t] + P, 16 * q:16 * q + 16, :].rearrange("r y c -> r (y c)"))\
                      .then_inc(xin[q % RING], 16)

            def load_modes(e):
                sp.dma_start(Ys[:], d["y1"][e]).then_inc(sem["ys_in"], 16)

            def sample(e, more):
                for q in range(NQ):
                    sp.wait_ge(sem["f_done"], e * (2 * NQ) + (2 * q + 2))
                    if q + RING < NQ:
                        load(e, q + RING)
                    elif more:
                        load(e + 1, q + RING - NQ)
                    if q == 0 and more:
                        load_modes(e + 1)

            load_modes(0)
            for q in range(RING):
                load(0, q)
            with sp.Fori(0, B - 1) as e:
                sample(e, True)
            sample(B - 1, False)

        @block.gpsimd
        def _(pool):
            pool.memset(half[:], -0.5).then_inc(sem["setup"], 1)
            pool.wait_ge(sem["setup"], 1)
            with pool.Fori(0, B) as e:
                for k in range(2):
                    pool.wait_ge(sem["half_ready"], e * 2 + (k + 1))
                    for t in range(T):
                        r0 = t * (H // 2)
                        pool.dma_start(d["x2"][e, k, r0:r0 + H // 2], XO[ONCE[t], k, t]).then_inc(stored[k], 16)
                pool.wait_ge(sem["root_in"], e + 1)
                pool.tensor_tensor(st.rs[:], st.var[:], half[:], ALU.pow).then_inc(sem["root_out"], 1)
            for k in range(2):
                pool.wait_ge(stored[k], B * 32)

        @block.tensor
        def _(pe):
            def body(e, prev):
                if e is not None:
                    pe.wait_ge(sem["ys_ready"], e + 1)
                    for k in range(4):
                        if k > 1:
                            pe.wait_ge(sem["tev_done"], e * 4 + (k - 1))
                        else:
                            after(pe, sem["vev_done"], e * 16)
                        for j in range(4):
                            ap = 4 * k + j
                            last = pe.transpose(PS[0:C, k % 2, j * P:j * P + P], Ys[:, ap * C:ap * C + C], ident[:])
                        last.then_inc(sem["tps_ready"], 1)
                    pe.wait_ge(sem["tev_done"], e * 4 + 4)
                    for cp in range(16):
                        pe.wait_ge(sem["vev_done"], e * 16 + (cp - 1)) if cp > 1 else None
                        for k in range(2):
                            last = pe.matmul(PS[0:64, cp % 2, k * W:k * W + W],
                                             UT[:].rearrange("b a (q c) -> b (a q) c", c=C)[:, :, 2 * cp + k],
                                             Di[:], start=True, stop=True)
                        last.then_inc(sem["vps_ready"], 1)
                if prev is not None:
                    pe.wait_ge(sem["st_in"], prev * 2 + 1)
                    st.pe_mean(pe, ST, once, lambda s: s % T, sem["st_out"])
                    pe.wait_ge(sem["st_in"], prev * 2 + 2)
                    st.pe_variance(pe, ST, once, lambda s: s % T, sem["st_out"])
                if e is None:
                    return

                def turn_x(n):
                    q, t = divmod(n, T)
                    if t == 0:
                        pe.wait_ge(xin[q % RING], e * 64 + (32 * (q // RING) + 32))
                    after(pe, sem["xt_done"], e * 28 + (n - 1))
                    for j in range(4):
                        last = pe.transpose(PS[:, 2 + n % 2, j * P:j * P + P],
                                            XC[:, q % RING, t, j * P:j * P + P], ident[:])
                    last.then_inc(sem["xt_ready"], 1)

                def row_sums(n):
                    q, t = divmod(n, T)
                    after(pe, sem["f_done"], e * 28 + (n - 1))
                    pe.matmul(PS[:, 4 + n % 2, :], Gr[:, t, :],
                              V[:, 16 * q:16 * q + 16, :].rearrange("a y c -> a (y c)"), start=True, stop=False)
                    pe.wait_ge(sem["xt_done"], e * 28 + (n + 1))
                    for j in range(4):
                        last = pe.matmul(PS[:, 4 + n % 2, j * P:j * P + P], XT[:, n % 2, j * P:j * P + P], Ws[:],
                                         start=False, stop=(j == 3))
                    last.then_inc(sem["f_ready"], 1)

                turn_x(0)
                pe.wait_ge(sem["vev_done"], e * 16 + 16)
                pe.wait_ge(sem["w_ready"], e + 1)
                for n in range(2 * NQ):
                    if n + 1 < 2 * NQ:
                        turn_x(n + 1)
                    row_sums(n)

            pe.wait_ge(sem["const_in"], 7 * 16)
            pe.matmul(ST[0:C, 128:128 + B], WT[:], keep.bcol1[0:C, :], start=True, stop=True)\
              .then_inc(sem["cst_in"], 1)
            turns(pe, body)

        @block.scalar
        def _(act):
            with act.Fori(0, B) as e:
                for k in range(4):
                    act.wait_ge(sem["tps_ready"], e * 4 + (k + 1))
                    act.activation(UT[:, 4 * k:4 * k + 4, :].rearrange("b a m -> b (a m)"), PS[0:C, k % 2, :],
                                   ACT.Copy).then_inc(sem["tev_done"], 1)
                for cp in range(16):
                    act.wait_ge(sem["vps_ready"], e * 16 + (cp + 1))
                    act.activation(V[:, :, 2 * cp:2 * cp + 2].rearrange("a y c -> a c y"),
                                   PS[0:64, cp % 2, 0:2 * W].rearrange("a (c y) -> a c y", c=2), ACT.Copy)\
                       .then_inc(sem["vev_done"], 1)
                for n in range(2 * NQ):
                    act.wait_ge(sem["xt_ready"], e * 28 + (n + 1))
                    if n >= 2:
                        act.wait_ge(sem["f_ready"], e * 28 + (n - 1))
                    act.activation(XT[:, n % 2, :], PS[:, 2 + n % 2, :], ACT.Copy).then_inc(sem["xt_done"], 1)

        @block.vector
        def _(dve):
            steps = Steps(dve, sem["dve_step"])
            dve.wait_ge(sem["const_in"], 7 * 16)
            dve.wait_ge(sem["cst_in"], 1)
            steps.done(dve.tensor_scalar(cst[:], ST[0:C, 128:128 + B], bias[:, 0:1], float(W), ALU.add, ALU.mult))
            steps.settle()

            def body(e, prev):
                if e is not None:
                    dve.wait_ge(sem["ys_in"], e * 16 + 16)
                    dve.tensor_tensor(Ys[0:C, 0:1], Ys[0:C, 0:1], cst[:, bass.ds(e, 1)], ALU.add)\
                       .then_inc(sem["ys_ready"], 1)
                    after(dve, sem["f_ready"], e * 28)
                    dve.tensor_scalar(Ws[:], Wbd[:], keep.acol1[:, bass.ds(e, 1)], None, ALU.mult)\
                       .then_inc(sem["w_ready"], 1)
                if prev is not None:
                    dve.wait_ge(sem["st_out"], prev * 2 + 1)
                    st.dve_deviations(dve, steps, ST, sem["st_in"])
                    dve.wait_ge(sem["st_out"], prev * 2 + 2)
                    st.dve_variance(dve, steps, ST, sem["root_in"])
                    dve.wait_ge(sem["root_out"], prev + 1)
                    st.dve_scales(dve, steps)
                    steps.done(dve.tensor_copy(keep.ab2[:, bass.ds(prev, 1), :].squeeze(1),
                                               st.ab[:].rearrange("p k g j -> p (k g j)")))
                if e is None:
                    return
                for n in range(2 * NQ):
                    q, t = divmod(n, T)
                    k, y0 = q // 7, 16 * (q % 7)
                    if n % 14 == 0:
                        after(dve, stored[k], e * 32)
                    dve.wait_ge(sem["f_ready"], e * 28 + (n + 1))
                    dve.scalar_tensor_tensor(
                        out=XO[:, k, t, :, y0:y0 + 16].rearrange("p c y -> p y c"),
                        in0=PS[:, 4 + n % 2, :].rearrange("p (y c) -> p y c", c=C), scalar=0.0,
                        in1=XC[:, q % RING, t].rearrange("p (y c) -> p y c", c=C), op0=ALU.max, op1=ALU.add)\
                       .then_inc(sem["f_done"], 1)
                    if n % 14 == 13:
                        dve.wait_ge(sem["f_done"], e * 28 + (n + 1))
                        for tt in range(T):
                            for g in range(G):
                                last = dve.bn_stats(st.bn[:, 2 * k + tt, g, :],
                                                    XO[:, k, tt, 2 * g:2 * g + 2, :].rearrange("p c y -> p (c y)"))
                                if tt == 1 and g == G - 1 and k == 0:
                                    last.then_inc(sem["half_ready"], 1)
                        if k == 1:
                            last.then_inc(sem["st_in"], 1)
                            steps.done(dve.memset(st.t1[:, 0:1], 0.0))
                            steps.settle()
                            dve.memset(st.t2[:, 0:1], 0.0).then_inc(sem["half_ready"], 1)

            turns(dve, body, steps, per_turn=keep.steps_c)


def pass_conv(nc, B, d, keep):
    KS = 7
    NWP = W + KS - 1
    with Scope(nc, "d_") as z:
        Bd = z.sb("Bd", [P, C * KS, P])
        X2 = z.sb("X2", [P, 4, T, CG, W])
        N2 = z.sb("N2", [P, 4, T, NWP])
        Rl = z.sb("R", [P, 2, T, W])
        X3 = z.sb("X3", [P, 2, CG, T, W])
        Zs = z.sb("Zs", [HALF, 2, P * C])
        SO = z.sb("SO", [P, 2, 512])
        Fr = z.sb("F", [P, T, P])
        Dc = z.sb("D", [HALF, 2, 64])
        once = z.sb("once", [P, T, P])
        b2 = z.sb("b2", [P, C])
        cf = z.sb("cf", [P, 2, C])
        half = z.sb("half", [P, G])
        one = z.sb("one", [1, 1])
        credit = z.sb("credit", [1, 3])
        rows4 = z.sb("rows4", [1, 2, P])
        st = GroupStats(z.sb, "st", T, W, ahead=True)
        PS = z.ps("PS", [P, 8, 512])
        ST = PS[:, 7, :]
        names = ("const_in", "setup", "n2_ready", "conv_ready", "relu_ready", "x3_ready", "zps_ready", "zev_done",
                 "modes_ready", "modes_out", "mst0", "mst1", "st_in", "st_out", "root_in", "root_out",
                 "dve_step", "act_step", "out0", "out1")
        sem = {n: z.sem(n) for n in names}
        xin = [z.sem(f"xin{k}") for k in range(4)]
        out_ = (sem["out0"], sem["out1"])
        mst = (sem["mst0"], sem["mst1"])
        NCONST = 5
        block = z.enter_context(nc.Block())

        def turns(engine, body, steps=None, per_turn=0):
            body(0, None)
            with engine.Fori(1, B) as e:
                if steps:
                    steps.enter(e - 1, per_turn)
                body(e, e - 1)
            if steps:
                steps.leave(B - 1)
            body(None, B - 1)

        @block.sync
        def _(sp):
            def load(e, cg):
                for t in range(T):
                    for k in range(2):
                        sp.dma_start(X2[:, cg % 4, t, :, k * HALF:(k + 1) * HALF],
                                     d["x2"][e, k, ROW0[t]:ROW0[t] + P, cg * CG:cg * CG + CG, :])\
                          .then_inc(xin[cg % 4], 16)

            def sample(e, more):
                for cg in range(NCG):
                    sp.wait_ge(sem["x3_ready"], e * C + (cg + 1) * CG)
                    for t in range(T):
                        r0 = t * (H // 2)
                        sp.dma_start(d["x3"][e, r0:r0 + H // 2, cg * CG:cg * CG + CG, :], X3[ONCE[t], cg % 2, :, t, :])\
                          .then_inc(out_[cg % 2], 16)
                    if cg < 4:
                        load(e, cg + 4)
                    elif more:
                        load(e + 1, cg - 4)

            for dst, src in ((Fr, d["F3"]), (Dc, d["D3"]), (once, d["once1"])):
                sp.dma_start(dst[:], src).then_inc(sem["const_in"], 16)
            sp.dma_start(b2[:], d["b2"].rearrange("(a c) -> a c", a=1).to_broadcast([P, C])).then_inc(sem["const_in"], 16)
            for cg in range(4):
                load(0, cg)
            sp.dma_start(Bd[:].rearrange("p n m -> p (n m)"), d["bands"]).then_inc(sem["const_in"], 16)
            with sp.Fori(0, B - 1) as e:
                sample(e, True)
            sample(B - 1, False)
            for k in range(2):
                sp.wait_ge(out_[k], B * 4 * 32)

        @block.gpsimd
        def _(pool):
            pool.memset(half[:], -0.5)
            pool.memset(one[:], 1.0)
            pool.memset(N2[:], 0.0).then_inc(sem["setup"], 1)
            for k, (name, count) in enumerate((("modes_out", 1), ("mst0", 16), ("mst1", 16))):
                pool.memset(credit[:, k:k + 1], 0.0).then_inc(sem[name], count)
            pool.wait_ge(sem["setup"], 1)
            with pool.Fori(0, B) as e:
                pool.wait_ge(sem["root_in"], e + 1)
                pool.tensor_tensor(st.rs[:], st.var[:], half[:], ALU.pow).then_inc(sem["root_out"], 1)

        @block.tensor
        def _(pe):
            def conv(e, c):
                pe.wait_ge(sem["n2_ready"], e * C + (c + 1))
                after(pe, sem["relu_ready"], e * C + (c - 1))
                for dy in range(KS):
                    last = pe.matmul(PS[:, c % 2, 0:2 * W], Bd[:, c * KS + dy, :], N2[:, c % 4, :, dy:dy + W],
                                     start=(dy == 0), stop=(dy == KS - 1))
                last.then_inc(sem["conv_ready"], 1)

            def over_rows(e, cg):
                pe.wait_ge(sem["x3_ready"], e * C + (cg + 1) * CG)
                after(pe, sem["zev_done"], e * NCG + (cg - 1))
                for yc in range(2):
                    for k in range(CG):
                        for t in range(T):
                            last = pe.matmul(PS[0:HALF, 2 + 2 * (cg % 2) + yc, k * P:k * P + P],
                                             X3[:, cg % 2, k, t, yc * HALF:(yc + 1) * HALF], Fr[:, t, :],
                                             start=(t == 0), stop=(t == T - 1))
                last.then_inc(sem["zps_ready"], 1)

            def over_columns(e, quarter):
                if quarter == 0:
                    pe.wait_ge(sem["zev_done"], e * NCG + NCG)
                after(pe, sem["modes_out"], e * 4 + (quarter + 1))
                for j in range(8):
                    ap = 8 * quarter + j
                    for yc in range(2):
                        last = pe.matmul(PS[:, 6, j * 64:j * 64 + 64], Zs[:, yc, ap * P:ap * P + P], Dc[:, yc, :],
                                         start=(yc == 0), stop=(yc == 1))
                last.then_inc(sem["modes_ready"], 1)

            def body(e, prev):
                for c in range(C):
                    if e is not None:
                        conv(e, c)
                    if prev is not None:
                        if c == 1:
                            over_rows(prev, NCG - 1)
                        if 2 <= c <= 5:
                            over_columns(prev, c - 2)
                        if c == 8:
                            pe.wait_ge(sem["st_in"], prev * 3 + 1)
                            st.pe_mean(pe, ST, once, lambda s: s, sem["st_out"])
                        if c == 10:
                            pe.wait_ge(sem["st_in"], prev * 3 + 2)
                            st.pe_variance(pe, ST, once, lambda s: s, sem["st_out"])
                        if c == 14:
                            pe.wait_ge(sem["st_in"], prev * 3 + 3)
                            on_columns(pe, ST, rows4, one, sem["st_out"])
                    if e is not None and c % 4 == 1 and c > 4:
                        over_rows(e, c // 4 - 1)

            pe.wait_ge(sem["const_in"], NCONST * 16)
            pe.wait_ge(sem["setup"], 1)
            turns(pe, body)

        @block.scalar
        def _(act):
            def keep_rows_done(e, cg):
                if cg == 0:
                    after(act, sem["modes_ready"], e * 4)
                act.wait_ge(sem["zps_ready"], e * NCG + (cg + 1))
                for yc in range(2):
                    last = act.activation(Zs[:, yc].rearrange("p (q c) -> p c q", c=C)[:, CG * cg:CG * cg + CG, :],
                                          PS[0:HALF, 2 + 2 * (cg % 2) + yc, :].rearrange("p (c q) -> p c q", c=CG),
                                          ACT.Copy)
                last.then_inc(sem["zev_done"], 1)

            def keep_modes(e, quarter):
                k = quarter % 2
                act.wait_ge(sem["modes_ready"], e * 4 + (quarter + 1))
                after(act, mst[k], e * 32 + (16 * (quarter // 2) + 16))
                act.activation(SO[:, k, :], PS[:, 6, :], ACT.Copy).then_inc(sem["modes_out"], 1)
                act.wait_ge(sem["modes_out"], e * 4 + (quarter + 2))
                act.dma_start(d["spec3"][e, :, quarter * 512:quarter * 512 + 512], SO[:, k, :]).then_inc(mst[k], 16)

            def body(e, prev):
                for c in range(C):
                    if prev is not None:
                        if c == 2:
                            keep_rows_done(prev, NCG - 1)
                        if 3 <= c <= 6:
                            keep_modes(prev, c - 3)
                    if e is not None and c % 4 == 2 and c > 5:
                        keep_rows_done(e, c // 4 - 1)
                    if e is not None:
                        act.wait_ge(sem["conv_ready"], e * C + (c + 1))
                        after(act, sem["x3_ready"], e * C + (c - 1))
                        act.activation(Rl[:, c % 2].rearrange("p t y -> p (t y)"), PS[:, c % 2, 0:2 * W], ACT.Relu,
                                       scale=2.25, bias=b2[:, c:c + 1]).then_inc(sem["relu_ready"], 1)

            act.wait_ge(sem["setup"], 2)
            turns(act, body)
            for k in range(2):
                act.wait_ge(mst[k], B * 32 + 16)

        @block.vector
        def _(dve):
            steps = Steps(dve, sem["dve_step"])
            dve.wait_ge(sem["const_in"], NCONST * 16)
            dve.wait_ge(sem["setup"], 1)
            dve.tensor_scalar(b2[:], b2[:], 2.25, None, ALU.mult).then_inc(sem["setup"], 1)

            def norm(e, c):
                cg, k = divmod(c, CG)
                if k == 0:
                    dve.wait_ge(xin[cg % 4], e * 128 + 64 * (cg // 4) + 64)
                after(dve, sem["conv_ready"], e * C + (c - 3))
                dve.tensor_scalar(N2[:, c % 4, :, 3:3 + W], X2[:, cg % 4, :, k, :], cf[:, 0, c:c + 1],
                                  cf[:, 1, c:c + 1], ALU.mult, ALU.add).then_inc(sem["n2_ready"], 1)

            def body(e, prev):
                if e is not None:
                    steps.done(dve.tensor_copy(cf[:].rearrange("p k c -> p (k c)"),
                                               keep.ab2[:, bass.ds(e, 1), :].squeeze(1)))
                    steps.settle()
                    norm(e, 0)
                    norm(e, 1)
                for c in range(C):
                    cg, k = divmod(c, CG)
                    if prev is not None:
                        if c == 8:
                            dve.wait_ge(sem["st_out"], prev * 3 + 1)
                            st.dve_deviations(dve, steps, ST, sem["st_in"])
                        if c == 10:
                            dve.wait_ge(sem["st_out"], prev * 3 + 2)
                            st.dve_variance(dve, steps, ST, sem["root_in"])
                        if c == 12:
                            dve.wait_ge(sem["root_out"], prev + 1)
                            st.dve_scales(dve, steps)
                            for j in range(2):
                                last = dve.tensor_copy(rows4[0:1, j].rearrange("p (q c) -> p q c", c=C),
                                                       st.row(j)[0:1].unsqueeze(1).to_broadcast([1, 4, C]))
                            last.then_inc(sem["st_in"], 1)
                        if c == 14:
                            dve.wait_ge(sem["st_out"], prev * 3 + 3)
                            steps.done(dve.tensor_copy(keep.acol3[:, bass.ds(prev, 1)], ST[:, 64:65]))
                            steps.done(dve.tensor_copy(keep.bcol3[:, bass.ds(prev, 1)], ST[:, 65:66]))
                    if e is None:
                        continue
                    if c + 2 < C:
                        norm(e, c + 2)
                    if k == 0:
                        after(dve, out_[cg % 2], e * 128 + 32 * (cg // 2))
                        after(dve, sem["zps_ready"], e * NCG + (cg - 1))
                    dve.wait_ge(sem["relu_ready"], e * C + (c + 1))
                    dve.tensor_tensor(X3[:, cg % 2, k], Rl[:, c % 2], X2[:, cg % 4, :, k, :], ALU.add)\
                       .then_inc(sem["x3_ready"], 1)
                    if c % 2:
                        dve.wait_ge(sem["x3_ready"], e * C + (c + 1))
                        for t in range(T):
                            last = dve.bn_stats(st.rows[:, t, c // 2, :], X3[:, cg % 2, k - 1:k + 1, t, :])
                        if c == C - 1:
                            st.hand_over(dve, steps, last, sem["st_in"])

            turns(dve, body, steps, per_turn=keep.steps_d)


def pass_inverse(nc, B, d, keep):
    R = H // 2
    with Scope(nc, "e_") as z:
        X3 = z.sb("X3", [R, 4, T, CG, W])
        OUT = z.sb("OUT", [R, 2, T, W, C])
        Ys = z.sb("Ys", [P, 2048])
        UT = z.sb("UT", [64, 32, P])
        V = z.sb("V", [P, 4, 2 * W])
        Di = z.sb("Di", [64, W])
        Gr = z.sb("G", [P, T, R])
        ident = z.sb("ident", [P, P])
        idle = z.sb("idle", [P, P], mybir.dt.bfloat16)
        PS = z.ps("PS", [P, 8, 512])
        names = ("const_in", "idle_set", "ys_in", "tps_ready", "tev_a", "tev_v", "vps_ready", "vev_done", "f_ready", "f_done",
                 "out0", "out1")
        sem = {n: z.sem(n) for n in names}
        xin = [z.sem(f"xin{k}") for k in range(4)]
        out_ = (sem["out0"], sem["out1"])
        block = z.enter_context(nc.Block())

        @block.sync
        def _(sp):
            def load(e, cg):
                for t in range(T):
                    sp.dma_start(X3[:, cg % 4, t], d["x3"][e, t * R:t * R + R, cg * CG:cg * CG + CG, :])\
                      .then_inc(xin[cg % 4], 16)

            def sample(e, more):
                for cg in range(NCG):
                    sp.wait_ge(sem["f_done"], e * 16 + (2 * cg + 2))
                    if cg == 0 and more:
                        sp.dma_start(Ys[:], d["y3"][e + 1]).then_inc(sem["ys_in"], 16)
                    if cg < 4:
                        load(e, cg + 4)
                    elif more:
                        load(e + 1, cg - 4)

            for dst, src in ((ident, d["ident"]), (Di, d["Di3"]), (Gr, d["G3"])):
                sp.dma_start(dst[:], src).then_inc(sem["const_in"], 16)
            sp.dma_start(Ys[:], d["y3"][0]).then_inc(sem["ys_in"], 16)
            for cg in range(4):
                load(0, cg)
            with sp.Fori(0, B - 1) as e:
                sample(e, True)
            sample(B - 1, False)

        @block.tensor
        def _(pe):
            pe.wait_ge(sem["const_in"], 48)
            pe.wait_ge(sem["idle_set"], 1)
            with pe.Fori(0, B) as e:
                pe.wait_ge(sem["ys_in"], e * 16 + 16)
                pe.ldweights(idle[:], tile_position=(0, 0))
                for k in range(8):
                    if k >= 2:
                        pe.wait_ge(sem["tev_a" if k % 2 == 0 else "tev_v"], e * 4 + k // 2)
                        pe.ldweights(idle[:], tile_position=(0, 0))
                    for j in range(4):
                        ap = 4 * k + j
                        last = pe.transpose(PS[0:64, k % 2, j * P:j * P + P], Ys[:, ap * 64:ap * 64 + 64], ident[:])
                    last.then_inc(sem["tps_ready"], 1)
                pe.wait_ge(sem["tev_a"], e * 4 + 4)
                pe.wait_ge(sem["tev_v"], e * 4 + 4)

                def over_columns(cp):
                    if cp >= 2:
                        pe.wait_ge(sem["vev_done"], e * 16 + (cp - 1))
                    for k in range(2):
                        last = pe.matmul(PS[:, 2 + cp % 2, k * W:k * W + W],
                                         UT[:].rearrange("b a (q c) -> b (a q) c", c=C)[:, :, 2 * cp + k], Di[:],
                                         start=True, stop=True)
                    last.then_inc(sem["vps_ready"], 1)

                over_columns(0)
                for cp in range(16):
                    if cp < 15:
                        over_columns(cp + 1)
                    pe.wait_ge(sem["vev_done"], e * 16 + (cp + 1))
                    if cp >= 2:
                        pe.wait_ge(sem["f_done"], e * 16 + (cp - 1))
                    for t in range(T):
                        last = pe.matmul(PS[0:R, 4 + 2 * (cp % 2) + t, 0:2 * W], Gr[:, t, :], V[:, cp % 4, :],
                                         start=True, stop=True)
                    last.then_inc(sem["f_ready"], 1)
                pe.wait_ge(sem["f_done"], e * 16 + 16)

        @block.scalar
        def _(act):
            with act.Fori(0, B) as e:
                for k in range(0, 8, 2):
                    act.wait_ge(sem["tps_ready"], e * 8 + (k + 1))
                    act.activation(UT[:, 4 * k:4 * k + 4, :].rearrange("b a m -> b (a m)"), PS[0:64, 0, :],
                                   ACT.Copy).then_inc(sem["tev_a"], 1)
                for cp in range(16):
                    act.wait_ge(sem["vps_ready"], e * 16 + (cp + 1))
                    if cp >= 4:
                        act.wait_ge(sem["f_ready"], e * 16 + (cp - 3))
                    act.activation(V[:, cp % 4, :], PS[:, 2 + cp % 2, 0:2 * W], ACT.Copy).then_inc(sem["vev_done"], 1)

        @block.vector
        def _(dve):
            def pair(i):
                for par in range(2):
                    e8 = i * 16 + 8 * par
                    e16 = i * 32 + 16 * par
                    for k in range(1, 8, 2):
                        dve.wait_ge(sem["tps_ready"], e8 + (k + 1))
                        dve.tensor_copy(UT[:, 4 * k:4 * k + 4, :].rearrange("b a m -> b (a m)"), PS[0:64, 1, :])\
                           .then_inc(sem["tev_v"], 1)
                    after(dve, out_[par], i * 32)
                    for cp in range(16):
                        cg, k = divmod(cp, 2)
                        if k == 0:
                            dve.wait_ge(xin[cg % 4], i * 128 + (64 * par + 32 * (cg // 4) + 32))
                        dve.wait_ge(sem["f_ready"], e16 + (cp + 1))
                        for t in range(T):
                            last = dve.tensor_tensor(
                                OUT[:, par, t, :, 2 * cp:2 * cp + 2].rearrange("p y c -> p c y"),
                                PS[0:R, 4 + 2 * (cp % 2) + t, 0:2 * W].rearrange("p (c y) -> p c y", c=2),
                                X3[:, cg % 4, t, 2 * k:2 * k + 2, :], ALU.add)
                        last.then_inc(sem["f_done"], 1)

            pair(0)
            with dve.Fori(1, B // 2) as i:
                pair(i)

        @block.gpsimd
        def _(pool):
            pool.memset(idle[:], 0.0).then_inc(sem["idle_set"], 1)
            with pool.Fori(0, B // 2) as i:
                for par in range(2):
                    pool.wait_ge(sem["f_done"], i * 32 + (16 * par + 16))
                    for t in range(T):
                        pool.dma_start(d["out"][i * 2 + par, t * R:t * R + R], OUT[:, par, t]).then_inc(out_[par], 16)
            for par in range(2):
                pool.wait_ge(out_[par], (B // 2) * 32)


def tables():
    f = np.float64
    x = np.arange(H)
    rows = np.stack([ROW0[t] + np.arange(P) for t in range(T)])
    counts = np.zeros((T, P))
    for t in range(T):
        counts[t, ONCE[t]] = 1
    t = {}
    k = np.arange(P)[:, None]
    m = np.arange(P)[None, :]
    t["band"] = np.stack([(k >= m - (s // 2 - 1)) & (k <= m + s // 2) for s in SCALES], 1)
    for name, n in (("1", 32), ("3", 64)):
        hn = n // 2
        a = np.array([h * hn + ap for ap in range(hn) for h in range(2)], f)
        ang = 2 * np.pi * rows[:, :, None] * a / H
        fw = np.stack([np.cos(ang), -np.sin(ang)], -1).reshape(T, P, 2 * n) / np.sqrt(H)
        t["F" + name] = (fw * counts[:, :, None]).transpose(1, 0, 2)
        b = np.arange(n)[:, None]
        D = np.cos(np.pi * (x[None, :] + 0.5) * b / W) * np.where(b == 0, np.sqrt(1.0 / W), np.sqrt(2.0 / W))
        t["D" + name] = D.T.reshape(2, HALF, n).transpose(1, 0, 2)
        t["Di" + name] = D
        out_rows = rows if name == "1" else np.arange(H).reshape(T, H // 2)
        ang = 2 * np.pi * a[:, None, None] * out_rows[None] / H
        w = np.where(a == 0, 1.0, 2.0)[:, None, None] / np.sqrt(H)
        inv = np.stack([w * np.cos(ang), -w * np.sin(ang) * (a != 0)[:, None, None]], 1)
        t["G" + name] = inv.reshape(2 * n, T, -1)
    once = np.broadcast_to(counts.T[:, :, None] * ROWSTAT, (P, T, P))
    t["once1"], t["once2"] = once, once / 2
    t["ident"] = np.eye(P)
    return {key: np.ascontiguousarray(v, dtype=np.float32) for key, v in t.items()}


def mixing(Rr, Ri):
    n = Rr.shape[2]
    m = Rr.shape[3]
    re, im = (np.asarray(r).reshape(C, C, 2, n // 2, m).transpose(2, 1, 3, 4, 0) for r in (Rr, Ri))
    out = np.stack([np.concatenate([re, im], -1), np.concatenate([im, re], -1)], 1)
    return np.ascontiguousarray(out.reshape(P, n // 2 * m, 2 * C))


class Keep:
    pass


def program(nc, B, d):
    with Scope(nc, "k_") as z:
        keep = Keep()
        keep.steps_a, keep.steps_c, keep.steps_d = 198, 12, 14
        keep.acol1, keep.bcol1 = z.sb("acol1", [P, B]), z.sb("bcol1", [P, B])
        keep.acol3, keep.bcol3 = z.sb("acol3", [P, B]), z.sb("bcol3", [P, B])
        keep.ab2 = z.sb("ab2", [P, B, 2 * C])
        pass_fractal(nc, B, d, keep)
        mix_modes(nc, "b1_", B, 512, d, d["spec1"], d["y1"], d["R1"], keep.acol1, keep.bcol1)
        pass_spectral(nc, B, d, keep)
        pass_conv(nc, B, d, keep)
        mix_modes(nc, "b3_", B, 2048, d, d["spec3"], d["y3"], d["R3"], keep.acol3, keep.bcol3)
        pass_inverse(nc, B, d, keep)


def kernel(x, L0_conv_gamma, L0_conv_beta, L0_conv_moving_mean, L0_conv_moving_var, L1_conv_R_real, L1_conv_R_imag,
           L1_conv_W, L1_conv_b, L2_conv_W, L2_conv_b, L3_conv_R_real, L3_conv_R_imag):
    import concourse.bacc as bacc
    from concourse.bass_utils import run_bass_kernel_spmd

    B = x.shape[0]
    arrays = tables()
    arrays["x"] = np.ascontiguousarray(x)
    arrays["gamma"], arrays["beta"] = np.asarray(L0_conv_gamma), np.asarray(L0_conv_beta)
    arrays["mean"], arrays["var"] = np.asarray(L0_conv_moving_mean), np.asarray(L0_conv_moving_var)
    arrays["R1"] = mixing(L1_conv_R_real, L1_conv_R_imag)
    arrays["R3"] = mixing(L3_conv_R_real, L3_conv_R_imag)
    wt = np.ascontiguousarray(np.asarray(L1_conv_W).T)
    arrays["wt"] = wt
    wbd = np.zeros((P, P), np.float32)
    for k in range(4):
        wbd[k * C:k * C + C, k * C:k * C + C] = wt
    arrays["wbd"] = wbd
    arrays["b1"] = np.asarray(L1_conv_b).reshape(C, 1)
    arrays["b2"] = np.asarray(L2_conv_b)
    w2 = np.asarray(L2_conv_W)[:, :, 0, :]
    bands = np.zeros((P, C, 7, P), np.float32)
    for dx in range(7):
        lo, hi = max(0, dx - 3), min(P, P + dx - 3)
        k = np.arange(lo, hi)
        bands[k, :, :, k - dx + 3] = w2[dx].T[None]
    arrays["bands"] = bands.reshape(P, -1)

    nc = bacc.Bacc("TRN2", target_bir_lowering=False, num_devices=1, dynamic_dma_scratch_size=4096)
    d = {}
    for name, a in arrays.items():
        d[name] = nc.dram_tensor("in_" + name, a.shape, mybir.dt.from_np(a.dtype), kind="ExternalInput").ap()
    for name, shape in (("x1", (B, H, W, C)), ("x2", (B, 2, H, C, HALF)), ("x3", (B, H, C, W)),
                        ("spec1", (B, P, 512)), ("y1", (B, P, 512)), ("spec3", (B, P, 2048)), ("y3", (B, P, 2048))):
        d[name] = nc.dram_tensor("tmp_" + name, shape, F32).ap()
    d["out"] = nc.dram_tensor("out", (B, H, W, C), F32, kind="ExternalOutput").ap()
    program(nc, B, d)
    r = run_bass_kernel_spmd(nc, [{"in_" + k: v for k, v in arrays.items()}], core_ids=[0])
    return r.results[0]["out"]
```

```python
import numpy as np
import concourse.bass as bass
from concourse import mybir
from contextlib import ExitStack

F32 = mybir.dt.float32
ALU = mybir.AluOpType
ACT = mybir.ActivationFunctionType
AX = mybir.AxisListType

H = 224
W = 224
C = 32
G = 16
T = 2
P = 128
ROW0 = (0, H - P)
ONCE = (slice(0, H // 2), slice(P - H // 2, P))
HALF = W // 2
CG = 4
NCG = C // CG
GN_EPS = 1e-5
ROWSTAT = 1.0 / (2 * H)
NP = 4
NY = W // NP
NB = 9
RB = 26
PADR = 3
ROWS2 = RB * NB + 6
ROWS3 = RB * NB
PAD = 8
WP = 240
SCALES = (16, 8, 2, 4)
LEVEL = {2: 1, 4: 2, 8: 3, 16: 0}


class Steps:

    def __init__(self, engine, sem):
        self.engine, self.sem, self.base, self.k = engine, sem, 0, 0

    def done(self, instruction):
        instruction.then_inc(self.sem, 1)
        self.k += 1

    def settle(self):
        self.engine.wait_ge(self.sem, self.base + self.k)

    def enter(self, i, per_turn):
        self.start, self.per_turn = self.base + self.k, per_turn
        self.base, self.k = i * per_turn + self.start, 0

    def leave(self, turns):
        assert self.k == self.per_turn, (self.k, self.per_turn)
        self.base, self.k = self.start + self.per_turn * turns, 0


def after(engine, sem, count):
    if not isinstance(count, int) or count > 0:
        engine.wait_ge(sem, count)


class Sample:

    def __init__(self, i, off):
        self.e, self.par, self.use = i * 2 + off, off % 2, i + off // 2


class GroupStats:

    def __init__(self, sb, name, segments, count, ahead=False, rows=P):
        self.segments, self.count, self.nrows = segments, count, rows
        self.bn = sb(name + "_bn", [rows, segments, G, 6])
        self.rows = sb(name + "_rows", [rows, segments, G, 6]) if ahead else self.bn
        self.gm = sb(name + "_gm", [P, G])
        self.dev = sb(name + "_dev", [rows, segments, G, 2])
        self.var = sb(name + "_var", [P, G])
        self.rs = sb(name + "_rs", [P, G])
        self.t1 = sb(name + "_t1", [P, G])
        self.t2 = sb(name + "_t2", [P, G])
        self.ab = sb(name + "_ab", [P, 2, G, 2])

    def hand_over(self, dve, steps, last, sem):
        steps.done(last)
        steps.settle()
        dve.tensor_copy(self.bn[:].rearrange("p s g v -> p (s g v)"),
                        self.rows[:].rearrange("p s g v -> p (s g v)")).then_inc(sem, 1)

    def pe_mean(self, pe, st, once, tile_of, sem):
        for s in range(self.segments):
            last = pe.matmul(st[:, 0:C], once[:, tile_of(s), :], self.bn[:, s, :, 1:6:3],
                             start=(s == 0), stop=(s == self.segments - 1))
        last.then_inc(sem, 1)

    def dve_deviations(self, dve, steps, st, sem):
        steps.done(dve.tensor_reduce(self.gm[:], st[:, 0:C].rearrange("p (g k) -> p g k", k=2),
                                     axis=AX.X, op=ALU.add))
        steps.settle()
        for s in range(self.segments):
            last = dve.tensor_tensor(self.dev[:, s], self.bn[:, s, :, 1:6:3],
                                     self.gm[0:self.nrows].unsqueeze(2).to_broadcast([self.nrows, G, 2]), ALU.subtract)
        steps.done(last)
        steps.settle()
        flat = self.dev[:].rearrange("p s g k -> p (s g k)")
        steps.done(dve.tensor_tensor(flat, flat, flat, ALU.mult))
        steps.settle()
        pairs = self.dev[:].rearrange("p s g k -> p (s g) k")
        dve.scalar_tensor_tensor(out=pairs, in0=self.bn[:].rearrange("p s g v -> p (s g) v")[:, :, 2:6:3],
                                 scalar=1.0 / self.count, in1=pairs, op0=ALU.mult,
                                 op1=ALU.add).then_inc(sem, 1)

    def pe_variance(self, pe, st, once, tile_of, sem):
        for s in range(self.segments):
            last = pe.matmul(st[:, C:2 * C], once[:, tile_of(s), :], self.dev[:, s],
                             start=(s == 0), stop=(s == self.segments - 1))
        last.then_inc(sem, 1)

    def dve_variance(self, dve, steps, st, sem):
        steps.done(dve.tensor_reduce(self.t1[:], st[:, C:2 * C].rearrange("p (g k) -> p g k", k=2),
                                     axis=AX.X, op=ALU.add))
        steps.settle()
        dve.tensor_scalar(self.var[:], self.t1[:], GN_EPS, None, ALU.add).then_inc(sem, 1)

    def dve_scales(self, dve, steps):
        newton(dve, steps, self.var[:], self.rs[:], self.t1[:], self.t2[:])
        steps.done(dve.scalar_tensor_tensor(out=self.t2[:], in0=self.gm[:], scalar=-1.0, in1=self.rs[:],
                                            op0=ALU.mult, op1=ALU.mult))
        steps.settle()
        dve.tensor_copy(self.ab[:, 0], self.rs[:].unsqueeze(2).to_broadcast([P, G, 2]))
        steps.done(dve.tensor_copy(self.ab[:, 1], self.t2[:].unsqueeze(2).to_broadcast([P, G, 2])))
        steps.settle()

    def row(self, k):
        return self.ab[:, k].rearrange("p g k -> p (g k)")


def newton(dve, steps, v, y, t1, t2):
    steps.done(dve.tensor_tensor(t1, y, y, ALU.mult))
    steps.settle()
    steps.done(dve.scalar_tensor_tensor(out=t2, in0=t1, scalar=-0.5, in1=v, op0=ALU.mult, op1=ALU.mult))
    steps.settle()
    steps.done(dve.tensor_scalar(t1, t2, 1.5, None, ALU.add))
    steps.settle()
    steps.done(dve.tensor_tensor(y, y, t1, ALU.mult))
    steps.settle()


def on_columns(pe, st, rows4, one, sem):
    for k in range(2):
        last = pe.matmul(st[:, 64 + k:65 + k], rows4[0:1, k, :], one[0:1, 0:1], start=True, stop=True)
    last.then_inc(sem, 1)


class Scope(ExitStack):

    def __init__(self, nc, prefix):
        super().__init__()
        self.nc, self.prefix = nc, prefix

    def sb(self, name, shape, dtype=F32):
        return self.enter_context(self.nc.sbuf_tensor(self.prefix + name, shape, dtype))

    def ps(self, name, shape):
        return self.enter_context(self.nc.psum_tensor(self.prefix + name, shape, F32))

    def sem(self, name):
        return self.enter_context(self.nc.semaphore(self.prefix + name))


def pass_fractal(nc, B, d, keep):
    UN = NCG * T
    with Scope(nc, "a_") as z:
        X = z.sb("X", [P, 2, T, W, C])
        Hb = z.sb("H", [P, 2, 4, CG, WP])
        L = z.sb("L", [P, 2, len(SCALES), CG, W])
        Zs = z.sb("Zs", [HALF, 2, 64 * C])
        SO = z.sb("SO", [P, 512])
        band = z.sb("band", [P, 4, P])
        Fr = z.sb("F", [P, T, 64])
        Dc = z.sb("D", [HALF, 2, 32])
        once = z.sb("once", [P, T, P])
        ident = z.sb("ident", [P, P])
        ones2 = z.sb("ones2", [2, P])
        half = z.sb("half", [P, C])
        eps = z.sb("eps", [P, 1])
        par4 = z.sb("par4", [P, 4, C])
        alp = z.sb("alp", [P, 2, C])
        mv = z.sb("mv", [P, 4, C])
        MM = z.sb("MM", [P, T, 2, C])
        mx = z.sb("mx", [P, 2, C])
        nm = z.sb("nm", [P, 2])
        ext = z.sb("ext", [2, 3])
        rng = z.sb("rng", [P, 4])
        credit = z.sb("credit", [1, 2])
        cf = z.sb("cf", [P, 2, 2, C])
        rows4 = z.sb("rows4", [1, 2, P])
        sx = GroupStats(z.sb, "sx", T, W)
        s1 = GroupStats(z.sb, "s1", T, W, ahead=True)
        PS = z.ps("PS", [P, 8, 512])
        STX, ST1 = PS[:, 7, 256:512], PS[:, 7, 0:256]

        names = ("const_in", "xs_ready", "h_ready", "m_ready", "ln_done", "t_ready",
                 "z_ready", "x1_ready", "zps_ready", "zev_done", "modes_ready", "modes_out", "modes_stored",
                 "coef_ready", "sx_in", "sx_out", "s1_in", "s1_out", "root_in", "root_out",
                 "dve_step", "setup")
        sem = {n: z.sem(n) for n in names}
        x_in = [[z.sem(f"x_in{k}{t}") for t in range(T)] for k in range(2)]
        x1_stored = [z.sem(f"x1_stored{t}") for t in range(T)]
        block = z.enter_context(nc.Block())

        def U(s, u):
            return s.e * UN + u

        def turns(body):
            body(None, None, Sample(0, 0))
            body(None, Sample(0, 0), Sample(0, 1))
            return (B - 2) // 2

        def looped(engine, body, steps=None, per_turn=0):
            n = turns(body)
            with engine.Fori(0, n) as i:
                if steps:
                    steps.enter(i, per_turn)
                body(Sample(i, 0), Sample(i, 1), Sample(i, 2))
                body(Sample(i, 1), Sample(i, 2), Sample(i, 3))
            if steps:
                steps.leave(n)
            body(Sample(n, 0), Sample(n, 1), None)
            body(Sample(n, 1), None, None)

        @block.sync
        def _(sp):
            for dst, src in ((band, d["band"]), (Fr, d["F1"]), (Dc, d["D1"]), (once, d["once1"]),
                             (ident, d["ident"])):
                sp.dma_start(dst[:], src).then_inc(sem["const_in"], 16)
            for k, name in enumerate(("gamma", "beta", "mean", "var")):
                sp.dma_start(par4[:, k, :], d[name].rearrange("(a c) -> a c", a=1).to_broadcast([P, C]))\
                  .then_inc(sem["const_in"], 16)

            def load(s, t):
                sp.dma_start(X[:, s.par, t], d["x"][s.e, ROW0[t]:ROW0[t] + P]).then_inc(x_in[s.par][t], 16)

            def finish(s, following):
                after(sp, sem["x1_ready"], U(s, UN))
                for t in range(T):
                    r0 = t * (H // 2)
                    sp.dma_start(d["x1"][s.e, r0:r0 + H // 2], X[ONCE[t], s.par, t])\
                      .then_inc(x1_stored[t], 16)
                if following is not None:
                    after(sp, sem["s1_in"], s.e * 3 + 1)
                    after(sp, sem["zps_ready"], s.e * NCG + NCG)
                    for t in range(T):
                        after(sp, x1_stored[t], s.e * 16 + 16)
                        load(following, t)
                after(sp, sem["modes_out"], s.e + 2)
                sp.dma_start(d["spec1"][s.e], SO[:]).then_inc(sem["modes_stored"], 16)

            for off in range(2):
                for t in range(T):
                    load(Sample(0, off), t)
            n = (B - 2) // 2
            with sp.Fori(0, n) as i:
                finish(Sample(i, 0), Sample(i, 2))
                finish(Sample(i, 1), Sample(i, 3))
            finish(Sample(n, 0), None)
            finish(Sample(n, 1), None)
            for t in range(T):
                sp.wait_ge(x1_stored[t], B * 16)
            sp.wait_ge(sem["modes_stored"], B * 16 + 16)

        @block.gpsimd
        def _(pool):
            pool.memset(ones2[:], 1.0)
            pool.memset(eps[:], 1e-7)
            pool.memset(Hb[:], 0.0)
            pool.memset(half[:], -0.5).then_inc(sem["setup"], 1)
            pool.memset(credit[:, 0:1], 0.0).then_inc(sem["modes_out"], 1)
            pool.memset(credit[:, 1:2], 0.0).then_inc(sem["modes_stored"], 16)

            def root(stats, k):
                pool.wait_ge(sem["root_in"], k)
                pool.tensor_tensor(stats.rs[:], stats.var[:], half[:, 0:G], ALU.pow).then_inc(sem["root_out"], 1)

            pool.wait_ge(sem["setup"], 1)
            pool.wait_ge(sem["root_in"], 1)
            pool.tensor_tensor(mv[:, 1], mv[:, 0], half[:], ALU.pow).then_inc(sem["root_out"], 1)
            root(sx, 2)
            root(sx, 3)
            with pool.Fori(0, B - 2) as i:
                root(s1, i * 2 + 4)
                root(sx, i * 2 + 5)
            root(s1, 2 * B)
            root(s1, 2 * B + 1)

        def root_count(s, of_x):
            if of_x:
                return s.e * 2 + 1 if not isinstance(s.e, int) or s.e >= 1 else 2
            return s.e * 2 + 4 if not isinstance(s.e, int) or s.e < B - 1 else 2 * B + 1

        @block.scalar
        def _(act):
            def scale(s, u):
                cg, t = divmod(u, T)
                if u == 0:
                    after(act, sem["coef_ready"], s.e + 1)
                    for j in range(T):
                        after(act, x_in[s.par][j], s.use * 16 + 16)
                after(act, sem["m_ready"], U(s, u) * 4 - 4)
                for k in range(CG):
                    c = cg * CG + k
                    last = act.activation(Hb[:, u % 2, 0, k, PAD:PAD + W], X[:, s.par, t, :, c], ACT.Relu,
                                          scale=cf[:, s.par, 0, c:c + 1], bias=cf[:, s.par, 1, c:c + 1])
                last.then_inc(sem["xs_ready"], 1)

            def logs(s, u):
                after(act, sem["x1_ready"], U(s, u) - 1)
                for j in range(4):
                    ch, sp_ = divmod(j, 2)
                    after(act, sem["m_ready"], U(s, u) * 4 + (j + 1))
                    out = L[:, u % 2, 2 * sp_:2 * sp_ + 2, 2 * ch:2 * ch + 2, :].rearrange("p s c y -> p s (c y)")
                    b0 = 2 * (j % 2)
                    act.activation(out, PS[:, b0:b0 + 2, 0:2 * W], ACT.Ln, bias=eps[:, 0:1])\
                       .then_inc(sem["ln_done"], 1)

            def affine(s, u):
                cg = u // T
                after(act, sem["t_ready"], U(s, u) + 1)
                for k in range(CG):
                    c = cg * CG + k
                    last = act.activation(L[:, u % 2, 2, k], L[:, u % 2, 0, k], ACT.Identity,
                                          scale=alp[:, 0, c:c + 1], bias=alp[:, 1, c:c + 1])
                last.then_inc(sem["z_ready"], 1)

            def keep_rows_done(s, cg):
                if cg == 0:
                    after(act, sem["modes_ready"], s.e)
                after(act, sem["zps_ready"], s.e * NCG + (cg + 1))
                for yc in range(2):
                    last = act.activation(
                        Zs[:, yc].rearrange("p (q c) -> p c q", c=C)[:, CG * cg:CG * cg + CG, :],
                        PS[0:HALF, 4 + cg % 2].rearrange("p (c y q) -> p c y q", c=CG, y=2)[:, :, yc],
                        ACT.Copy)
                last.then_inc(sem["zev_done"], 1)

            def body(prev, cur, nxt):
                for u in range(UN):
                    if u < UN - 1:
                        if cur:
                            scale(cur, u + 1)
                    elif nxt:
                        scale(nxt, 0)
                    if u == 0 and prev:
                        affine(prev, UN - 1)
                    if prev and u == 1:
                        keep_rows_done(prev, 6)
                    if prev and u == 2:
                        keep_rows_done(prev, 7)
                    if prev and u == 6:
                        after(act, sem["modes_ready"], prev.e + 1)
                        after(act, sem["modes_stored"], prev.e * 16 + 16)
                        act.activation(SO[:], PS[:, 6, :], ACT.Copy).then_inc(sem["modes_out"], 1)
                    if cur and u == 6:
                        keep_rows_done(cur, 0)
                    if cur and u >= 7 and u % 2 == 1:
                        keep_rows_done(cur, (u - 5) // 2)
                    if cur:
                        logs(cur, u)
                    if u > 0 and cur:
                        affine(cur, u - 1)

            act.wait_ge(sem["setup"], 2)
            looped(act, body)

        @block.tensor
        def _(pe):
            def boxes(s, u):
                after(pe, sem["h_ready"], U(s, u) + 1)
                for j in range(4):
                    ch, sp_ = divmod(j, 2)
                    after(pe, sem["ln_done"], U(s, u) * 4 + (j - 1))
                    for k in range(2):
                        pos = 2 * sp_ + k
                        last = pe.matmul(PS[:, 2 * (j % 2) + k, 0:2 * W], band[:, pos, :],
                                         Hb[:, u % 2, LEVEL[SCALES[pos]], 2 * ch:2 * ch + 2, PAD:PAD + W],
                                         start=True, stop=True)
                    last.then_inc(sem["m_ready"], 1)

            def over_rows(s, cg, part):
                after(pe, sem["x1_ready"], U(s, 2 * cg + 2))
                after(pe, sem["zev_done"], s.e * NCG + (cg - 1))
                for k in range(2 * part, 2 * part + 2):
                    for yc in range(2):
                        q0 = (k * 2 + yc) * 64
                        for t in range(T):
                            last = pe.matmul(PS[0:HALF, 4 + cg % 2, q0:q0 + 64],
                                             X[:, s.par, t, yc * HALF:(yc + 1) * HALF, cg * CG + k],
                                             Fr[:, t, :], start=(t == 0), stop=(t == T - 1))
                if part == 1:
                    last.then_inc(sem["zps_ready"], 1)

            def over_columns(s, aps):
                if aps[0] == 0:
                    after(pe, sem["zev_done"], s.e * NCG + NCG)
                    after(pe, sem["modes_out"], s.e + 1)
                for ap in aps:
                    for yc in range(2):
                        last = pe.matmul(PS[:, 6, ap * 32:ap * 32 + 32], Zs[:, yc, ap * P:ap * P + P],
                                         Dc[:, yc, :], start=(yc == 0), stop=(yc == 1))
                if aps[-1] == 15:
                    last.then_inc(sem["modes_ready"], 1)

            def body(prev, cur, nxt):
                for u in range(UN):
                    if cur:
                        boxes(cur, u)
                    if prev and u == 2:
                        after(pe, sem["s1_in"], prev.e * 3 + 1)
                        s1.pe_mean(pe, ST1, once, lambda s: s, sem["s1_out"])
                    if prev and u == 3:
                        after(pe, sem["s1_in"], prev.e * 3 + 2)
                        s1.pe_variance(pe, ST1, once, lambda s: s, sem["s1_out"])
                    if prev and u == 5:
                        after(pe, sem["s1_in"], prev.e * 3 + 3)
                        on_columns(pe, ST1, rows4, ones2, sem["s1_out"])
                    if nxt and u == 11:
                        after(pe, sem["sx_in"], nxt.e * 4 + 1)
                        sx.pe_mean(pe, STX, once, lambda s: s, sem["sx_out"])
                    if nxt and u == 12:
                        after(pe, sem["sx_in"], nxt.e * 4 + 2)
                        sx.pe_variance(pe, STX, once, lambda s: s, sem["sx_out"])
                    if nxt and u == 13:
                        after(pe, sem["sx_in"], nxt.e * 4 + 3)
                        pe.matmul(STX[0:2, 64:64 + P], nm[:], ident[:], start=True, stop=True)\
                          .then_inc(sem["sx_out"], 1)
                    if nxt and u == 14:
                        after(pe, sem["sx_in"], nxt.e * 4 + 4)
                        pe.matmul(STX[:, 192:194], ones2[:], ext[:, 1:3], start=True, stop=True)\
                          .then_inc(sem["sx_out"], 1)
                    if prev and 2 <= u <= 5:
                        over_columns(prev, range(4 * u - 8, 4 * u - 4))
                    if prev and u == 0:
                        over_rows(prev, 6, 1)
                    if prev and u == 1:
                        over_rows(prev, 7, 0)
                        over_rows(prev, 7, 1)
                    if cur and u >= 3:
                        over_rows(cur, (u - 3) // 2, (u - 3) % 2)

            pe.wait_ge(sem["const_in"], 9 * 16)
            pe.wait_ge(sem["setup"], 1)
            looped(pe, body)

        @block.vector
        def _(dve):
            steps = Steps(dve, sem["dve_step"])
            dve.wait_ge(sem["const_in"], 9 * 16)
            dve.wait_ge(sem["setup"], 1)
            dve.tensor_scalar(mv[:, 0], par4[:, 3], 0.001, None, ALU.add).then_inc(sem["root_in"], 1)
            dve.wait_ge(sem["root_in"], 1)
            dve.wait_ge(sem["root_out"], 1)
            newton(dve, steps, mv[:, 0], mv[:, 1], mv[:, 2], mv[:, 3])
            steps.done(dve.tensor_tensor(mv[:, 2], mv[:, 1], par4[:, 0], ALU.mult))
            steps.settle()
            steps.done(dve.tensor_tensor(mv[:, 3], mv[:, 2], par4[:, 2], ALU.mult))
            steps.settle()
            steps.done(dve.tensor_scalar(alp[:, 0], mv[:, 2], float(0.1 / np.log(2.0)), None, ALU.mult))
            steps.done(dve.tensor_tensor(alp[:, 1], par4[:, 1], mv[:, 3], ALU.subtract))
            steps.settle()
            dve.tensor_copy(mv[:, 0], mv[:, 1]).then_inc(sem["setup"], 1)

            def sums(s, u, level):
                h = Hb[:, u % 2]
                if level == 1:
                    after(dve, sem["xs_ready"], U(s, u) + 1)
                    after(dve, sem["m_ready"], U(s, u) * 4 - 4)
                    steps.done(dve.tensor_tensor(h[:, 1, :, 1:239], h[:, 0, :, 1:239], h[:, 0, :, 2:240], ALU.add))
                    return
                steps.settle()
                if level == 2:
                    steps.done(dve.tensor_tensor(h[:, 2, :, 2:238], h[:, 1, :, 1:237], h[:, 1, :, 3:239], ALU.add))
                elif level == 3:
                    steps.done(dve.tensor_tensor(h[:, 3, :, 4:236], h[:, 2, :, 2:234], h[:, 2, :, 6:238], ALU.add))
                else:
                    dve.tensor_tensor(h[:, 0, :, 8:232], h[:, 3, :, 4:228], h[:, 3, :, 12:236], ALU.add)\
                       .then_inc(sem["h_ready"], 1)

            def combine(s, u):
                after(dve, sem["ln_done"], U(s, u) * 4 + 4)
                lu = L[:, u % 2].rearrange("p s c y -> p s (c y)")
                steps.done(dve.tensor_tensor(lu[:, 0:2], lu[:, 0:2], lu[:, 2:4], ALU.subtract))
                steps.settle()
                dve.scalar_tensor_tensor(out=lu[:, 0], in0=lu[:, 0], scalar=3.0, in1=lu[:, 1],
                                         op0=ALU.mult, op1=ALU.add).then_inc(sem["t_ready"], 1)

            def add(s, u):
                cg, t = divmod(u, T)
                after(dve, sem["z_ready"], U(s, u) + 1)
                xv = X[:, s.par, t, :, cg * CG:cg * CG + CG].rearrange("p y c -> p c y")
                dve.tensor_tensor(xv, xv, L[:, u % 2, 2], ALU.add).then_inc(sem["x1_ready"], 1)

            def stats_of_x1(s, u, j):
                cg, t = divmod(u, T)
                if j == 0:
                    after(dve, sem["x1_ready"], U(s, u) + 1)
                g = 2 * cg + j
                last = dve.bn_stats(s1.rows[:, t, g, :], X[:, s.par, t, :, 2 * g:2 * g + 2])
                if u == UN - 1 and j == 1:
                    s1.hand_over(dve, steps, last, sem["s1_in"])

            def stats_of_x(s, k):
                t, cg = divmod(k, NCG)
                if cg == 0:
                    after(dve, x_in[s.par][t], s.use * 16 + 16)
                for g in (2 * cg, 2 * cg + 1):
                    dve.bn_stats(sx.bn[:, t, g, :], X[:, s.par, t, :, 2 * g:2 * g + 2])
                xv = X[:, s.par, t, :, cg * CG:cg * CG + CG].rearrange("p y c -> p c y")
                dve.tensor_reduce(MM[:, t, 0, cg * CG:cg * CG + CG], xv, axis=AX.X, op=ALU.max)
                last = dve.tensor_reduce(MM[:, t, 1, cg * CG:cg * CG + CG], xv, axis=AX.X, op=ALU.min)
                if k == 2 * NCG - 1:
                    last.then_inc(sem["sx_in"], 1)

            def extremes(s):
                steps.done(dve.tensor_tensor(mx[:, 0], MM[:, 0, 0], MM[:, 1, 0], ALU.max))
                steps.done(dve.tensor_tensor(mx[:, 1], MM[:, 0, 1], MM[:, 1, 1], ALU.min))
                steps.settle()
                steps.done(dve.tensor_tensor(mx[:, 0], mx[:, 0], sx.row(0), ALU.mult))
                steps.done(dve.scalar_tensor_tensor(out=mx[:, 1], in0=mx[:, 1], scalar=-1.0, in1=sx.row(0),
                                                    op0=ALU.mult, op1=ALU.mult))
                steps.settle()
                steps.done(dve.tensor_tensor(mx[:, 0], mx[:, 0], sx.row(1), ALU.add))
                steps.done(dve.tensor_tensor(mx[:, 1], mx[:, 1], sx.row(1), ALU.subtract))
                steps.settle()
                dve.tensor_reduce(nm[:], mx[:], axis=AX.X, op=ALU.max).then_inc(sem["sx_in"], 1)

            def body(prev, cur, nxt):
                for u in range(UN):
                    if prev and u == 3:
                        after(dve, sem["s1_out"], prev.e * 3 + 1)
                        s1.dve_deviations(dve, steps, ST1, sem["s1_in"])
                    if prev and u == 5:
                        after(dve, sem["root_out"], root_count(prev, False))
                        s1.dve_scales(dve, steps)
                        for k in range(2):
                            last = dve.tensor_copy(
                                rows4[0:1, k].rearrange("p (q c) -> p q c", c=C),
                                s1.row(k)[0:1].unsqueeze(1).to_broadcast([1, 4, C]))
                        last.then_inc(sem["s1_in"], 1)
                    if prev and u == 6:
                        after(dve, sem["s1_out"], prev.e * 3 + 3)
                        steps.done(dve.tensor_copy(keep.acol1[:, bass.ds(prev.e, 1)], ST1[:, 64:65]))
                        steps.done(dve.tensor_copy(keep.bcol1[:, bass.ds(prev.e, 1)], ST1[:, 65:66]))
                    if nxt and u == 12:
                        after(dve, sem["sx_out"], nxt.e * 4 + 1)
                        sx.dve_deviations(dve, steps, STX, sem["sx_in"])
                    if nxt and u == 14:
                        after(dve, sem["sx_out"], nxt.e * 4 + 3)
                        steps.done(dve.tensor_reduce(ext[:, 0:1], STX[0:2, 64:64 + P], axis=AX.X, op=ALU.max))
                        steps.settle()
                        dve.tensor_scalar(ext[:, 1:3], ident[0:2, 0:2], ext[:, 0:1], None, ALU.mult)\
                           .then_inc(sem["sx_in"], 1)
                    for level in range(1, 5):
                        if u < UN - 1:
                            if cur:
                                sums(cur, u + 1, level)
                        elif nxt:
                            sums(nxt, 0, level)
                        if u > 1 and cur and level <= 2:
                            stats_of_x1(cur, u - 2, level - 1)
                        if u < 2 and prev and level <= 2:
                            stats_of_x1(prev, UN - 2 + u, level - 1)
                    if nxt and u == 13:
                        after(dve, sem["root_out"], root_count(nxt, True))
                        sx.dve_scales(dve, steps)
                        extremes(nxt)
                    if cur:
                        combine(cur, u)
                    if u > 0 and cur:
                        add(cur, u - 1)
                    if u == 0 and prev:
                        add(prev, UN - 1)
                    if prev and u == 3:
                        after(dve, sem["s1_out"], prev.e * 3 + 2)
                        s1.dve_variance(dve, steps, ST1, sem["root_in"])
                    if nxt and u == 12:
                        after(dve, sem["sx_out"], nxt.e * 4 + 2)
                        sx.dve_variance(dve, steps, STX, sem["root_in"])
                    if nxt and 4 <= u <= 10:
                        for k in range(2 * (u - 4) + (u == 10), 2 * (u - 4) + 2 + (u >= 9) + (u == 10)):
                            stats_of_x(nxt, k)
                    if nxt and u == 14:
                        after(dve, sem["sx_out"], nxt.e * 4 + 4)
                        steps.done(dve.tensor_copy(rng[:, 0:2], STX[:, 192:194]))
                        steps.settle()
                        steps.done(dve.tensor_tensor(rng[:, 2:3], rng[:, 0:1], rng[:, 1:2], ALU.add))
                        steps.settle()
                        steps.done(dve.tensor_scalar(rng[:, 2:3], rng[:, 2:3], 1e-7, None, ALU.add))
                        steps.settle()
                        steps.done(dve.reciprocal(rng[:, 3:4], rng[:, 2:3]))
                        steps.settle()
                        steps.done(dve.tensor_scalar(cf[:, nxt.par, 0], sx.row(0), rng[:, 3:4], None, ALU.mult))
                        steps.settle()
                        dve.tensor_scalar(cf[:, nxt.par, 1], sx.row(1), rng[:, 1:2], rng[:, 3:4], ALU.add,
                                          ALU.mult).then_inc(sem["coef_ready"], 1)

            looped(dve, body, steps, per_turn=keep.steps_a)


def mix_modes(nc, name, B, pairs, d, spec, out, R, acol, bcol):
    SC = 128
    SLOTS = SC // 4
    n = pairs // SC
    with Scope(nc, name) as z:
        Rb = z.sb("R", [P, 2, SC, 64])
        Xb = z.sb("X", [P, 2, B, SC])
        XB = z.sb("XB", [P, 2, SC, 2, 16])
        Yb = z.sb("Y", [P, 2, SLOTS, 64])
        corr = z.sb("corr", [C, n, B])
        PS = z.ps("PS", [P, 8, 512])
        in_ = (z.sem("in0"), z.sem("in1"))
        out_ = (z.sem("out0"), z.sem("out1"))
        ready, mixed, low, high, step, blank = (z.sem(s) for s in ("ready", "mixed", "low", "high", "step", "blank"))
        block = z.enter_context(nc.Block())

        @block.sync
        def _(sp):
            def load(sc, par):
                sp.dma_start(Rb[:, par], R[:, bass.ds(sc * SC, SC), :]).then_inc(in_[par], 16)
                sp.dma_start(Xb[:, par], spec.rearrange("e p m -> p e m")[:, :, bass.ds(sc * SC, SC)])\
                  .then_inc(in_[par], 16)

            load(0, 0)
            load(1, 1)
            with sp.Fori(0, n // 2 - 1) as i:
                for par in range(2):
                    sp.wait_ge(mixed, i * 4 + (2 * par + 2))
                    load(i * 2 + (par + 2), par)

        @block.gpsimd
        def _(pool):
            pool.memset(XB[:], 0.0).then_inc(blank, 1)

        @block.vector
        def _(dve):
            dve.memset(corr[:], 0.0).then_inc(step, 1)
            dve.wait_ge(step, 1)
            dve.tensor_scalar(corr[:, 0, :], bcol[0:C, :], float(W), None, ALU.mult).then_inc(step, 1)
            dve.wait_ge(step, 2)
            dve.wait_ge(blank, 1)

            def prepare(sc, par, i):
                dve.wait_ge(in_[par], i * 32 + 32)
                for h in range(2):
                    neg = Rb[64 * h + 32:64 * h + 64, par, :, 0:32]
                    dve.tensor_scalar(neg, neg, -1.0, None, ALU.mult)
                    rows = slice(64 * h, 64 * h + 64)
                    last = dve.tensor_tensor(XB[rows, par, :, h, 0:B].rearrange("p m e -> p e m"), Xb[rows, par],
                                             acol[rows, :].unsqueeze(2).to_broadcast([64, B, SC]), ALU.mult)
                last.then_inc(step, 1)
                dve.wait_ge(step, i * 2 + (3 + par))
                dve.tensor_tensor(XB[0:C, par, 0, 0, 0:B], XB[0:C, par, 0, 0, 0:B],
                                  corr[:, bass.ds(sc, 1), :].squeeze(1), ALU.add).then_inc(ready, 1)

            def collect(i, par):
                after(dve, out_[par], i * 128)
                dve.wait_ge(mixed, i * 4 + (2 * par + 2))
                dve.tensor_copy(Yb[:, par, SLOTS // 2:].rearrange("p s v -> p (s v)"),
                                PS[:, 4 * par + 2:4 * par + 4, :].rearrange("p k v -> p (k v)")).then_inc(high, 1)

            def turn(i, more):
                for par in range(2):
                    if par == 0 or more:
                        prepare(i * 2 + (par + 1), 1 - par, i + par)
                    collect(i, par)

            prepare(0, 0, 0)
            turn(0, True)
            if n > 4:
                with dve.Fori(1, n // 2 - 1) as i:
                    turn(i, True)
            turn(n // 2 - 1, False)

        @block.tensor
        def _(pe):
            def turn(i):
                for par in range(2):
                    pe.wait_ge(ready, i * 2 + (par + 1))
                    after(pe, low, i * 2 + (par - 1))
                    after(pe, high, i * 2 + (par - 1))
                    for s in range(SLOTS):
                        for j in range(4):
                            m = SLOTS * j + s
                            last = pe.matmul(PS[32 * j:32 * j + 32, 4 * par + s // 8, (s % 8) * 64:(s % 8) * 64 + 64],
                                             XB[:, par, m].rearrange("p h e -> p (h e)"), Rb[:, par, m, :],
                                             start=True, stop=True)
                        if s % 16 == 15:
                            last.then_inc(mixed, 1)

            turn(0)
            with pe.Fori(1, n // 2) as i:
                turn(i)

        @block.scalar
        def _(act):
            def turn(i):
                for par in range(2):
                    after(act, out_[par], i * 128)
                    act.wait_ge(mixed, i * 4 + (2 * par + 1))
                    act.activation(Yb[:, par, 0:SLOTS // 2].rearrange("p s v -> p (s v)"),
                                   PS[:, 4 * par:4 * par + 2, :].rearrange("p k v -> p (k v)"), ACT.Copy)\
                       .then_inc(low, 1)
                    act.wait_ge(low, i * 2 + (par + 1))
                    act.wait_ge(high, i * 2 + (par + 1))
                    for j in range(4):
                        for h in range(2):
                            act.dma_start(out[:, h, bass.ds((i * 2 + par) * SC + SLOTS * j, SLOTS), :],
                                          Yb[32 * j + 16 * h:32 * j + 16 * h + B, par]).then_inc(out_[par], 16)

            turn(0)
            with act.Fori(1, n // 2) as i:
                turn(i)
            for par in range(2):
                act.wait_ge(out_[par], (n // 2) * 128)


def pass_spectral(nc, B, d, keep):
    NQ = W // 16
    RING = 7
    with Scope(nc, "c_") as z:
        XC = z.sb("XC", [P, RING, T, 16 * C])
        XO = z.sb("XO", [P, T, NP, C, NY])
        UT = z.sb("UT", [C, 16, 2, 64])
        V = z.sb("V", [64, W, C])
        XT = z.sb("XT", [P, 2, 512])
        Wbd = z.sb("Wbd", [P, P])
        Ws = z.sb("Ws", [P, P])
        WT = z.sb("WT", [C, C])
        bias = z.sb("bias", [1, C])
        cst = z.sb("cst", [1, B, C])
        zero = z.sb("zero", [16, NP * C * NY])
        Di = z.sb("Di", [C, W])
        Gr = z.sb("G", [64, T, P])
        once = z.sb("once", [P, T, P])
        ident = z.sb("ident", [P, P])
        half = z.sb("half", [P, G])
        st = GroupStats(z.sb, "st", T, W)
        PS = z.ps("PS", [P, 8, 512])
        ST = PS[:, 6, :]
        names = ("const_in", "setup", "cst_in", "ys_in", "ys_ready", "w_ready", "vps_ready", "vev_done",
                 "xt_ready", "xt_done", "f_ready", "f_done", "st_in", "st_out", "root_in", "root_out",
                 "dve_step", "stored", "pads")
        sem = {n: z.sem(n) for n in names}
        xin = [z.sem(f"xin{k}") for k in range(RING)]
        block = z.enter_context(nc.Block())

        def turns(engine, body, steps=None, per_turn=0):
            body(0, None, True)
            with engine.Fori(1, B - 1) as e:
                if steps:
                    steps.enter(e - 1, per_turn)
                body(e, e - 1, True)
            if steps:
                steps.leave(B - 2)
            body(B - 1, B - 2, False)
            body(None, B - 1, False)

        @block.sync
        def _(sp):
            for dst, src in ((Wbd, d["wbd"]), (WT, d["wt"]), (bias, d["b1"]), (Di, d["Di1"]), (Gr, d["G1"]),
                             (once, d["once1"]), (ident, d["ident"])):
                sp.dma_start(dst[:], src).then_inc(sem["const_in"], 16)

            def load(e, q):
                for t in range(T):
                    sp.dma_start(XC[:, q % RING, t],
                                 d["x1"][e, ROW0[t]:ROW0[t] + P, 16 * q:16 * q + 16, :].rearrange("r y c -> r (y c)"))\
                      .then_inc(xin[q % RING], 16)

            def load_modes(e):
                for h in range(2):
                    sp.dma_start(UT[:, :, h, :], d["y1"][e, h].rearrange("(a b) v -> b a v", b=C))\
                      .then_inc(sem["ys_in"], 16)

            def sample(e, more):
                for q in range(NQ):
                    sp.wait_ge(sem["f_done"], e * (2 * NQ) + (2 * q + 2))
                    if q + RING < NQ:
                        load(e, q + RING)
                    elif more:
                        load(e + 1, q + RING - NQ)
                    if q == 0 and more:
                        load_modes(e + 1)
                for t in range(T):
                    r0 = PADR + t * (H // 2)
                    sp.dma_start(d["x2"][e, r0:r0 + H // 2], XO[ONCE[t], t]).then_inc(sem["stored"], 16)

            load_modes(0)
            for q in range(RING):
                load(0, q)
            with sp.Fori(0, B - 1) as e:
                sample(e, True)
            sample(B - 1, False)
            sp.wait_ge(sem["stored"], B * 32)

        @block.gpsimd
        def _(pool):
            pool.memset(half[:], -0.5).then_inc(sem["setup"], 1)
            pool.memset(zero[:], 0.0).then_inc(sem["setup"], 1)
            pool.wait_ge(sem["setup"], 2)
            for r0, n in ((0, PADR), (PADR + H, ROWS2 - PADR - H)):
                for e in range(B):
                    pool.dma_start(d["x2"][e, r0:r0 + n].rearrange("r p c y -> r (p c y)"), zero[0:n, :])\
                        .then_inc(sem["pads"], 16)
            with pool.Fori(0, B) as e:
                pool.wait_ge(sem["root_in"], e + 1)
                pool.tensor_tensor(st.rs[:], st.var[:], half[:], ALU.pow).then_inc(sem["root_out"], 1)
            pool.wait_ge(sem["pads"], 2 * B * 16)

        @block.tensor
        def _(pe):
            def body(e, prev, more):
                if e is not None:
                    pe.wait_ge(sem["ys_ready"], e + 1)
                    for cp in range(16):
                        after(pe, sem["vev_done"], e * 16 + (cp - 1))
                        for k in range(2):
                            last = pe.matmul(PS[0:64, cp % 2, k * W:k * W + W],
                                             UT[:].rearrange("b a h (q c) -> b (a h q) c", c=C)[:, :, 2 * cp + k],
                                             Di[:], start=True, stop=True)
                        last.then_inc(sem["vps_ready"], 1)
                if prev is not None:
                    pe.wait_ge(sem["st_in"], prev * 2 + 1)
                    st.pe_mean(pe, ST, once, lambda s: s, sem["st_out"])
                if e is None:
                    pe.wait_ge(sem["st_in"], prev * 2 + 2)
                    st.pe_variance(pe, ST, once, lambda s: s, sem["st_out"])
                    return

                def turn_x(n):
                    q, t = divmod(n, T)
                    if t == 0:
                        pe.wait_ge(xin[q % RING], e * 64 + (32 * (q // RING) + 32))
                    after(pe, sem["xt_done"], e * 28 + (n - 1))
                    for j in range(4):
                        last = pe.transpose(PS[:, 2 + n % 2, j * P:j * P + P],
                                            XC[:, q % RING, t, j * P:j * P + P], ident[:])
                    last.then_inc(sem["xt_ready"], 1)

                def row_sums(n):
                    q, t = divmod(n, T)
                    after(pe, sem["f_done"], e * 28 + (n - 1))
                    pe.matmul(PS[:, 4 + n % 2, :], Gr[:, t, :],
                              V[:, 16 * q:16 * q + 16, :].rearrange("a y c -> a (y c)"), start=True, stop=False)
                    pe.wait_ge(sem["xt_done"], e * 28 + (n + 1))
                    for j in range(4):
                        last = pe.matmul(PS[:, 4 + n % 2, j * P:j * P + P], XT[:, n % 2, j * P:j * P + P], Ws[:],
                                         start=False, stop=(j == 3))
                    last.then_inc(sem["f_ready"], 1)

                turn_x(0)
                pe.wait_ge(sem["vev_done"], e * 16 + 16)
                pe.wait_ge(sem["w_ready"], e + 1)
                for n in range(2 * NQ):
                    if n + 1 < 2 * NQ:
                        turn_x(n + 1)
                    if n == 0 and prev is not None:
                        pe.wait_ge(sem["st_in"], prev * 2 + 2)
                        st.pe_variance(pe, ST, once, lambda s: s, sem["st_out"])
                    row_sums(n)

            pe.wait_ge(sem["const_in"], 7 * 16)
            for e in range(B):
                last = pe.matmul(PS[0:1, 5, e * C:e * C + C], keep.bcol1[0:C, e:e + 1], WT[:], start=True, stop=True)
            last.then_inc(sem["cst_in"], 1)
            turns(pe, body)

        @block.scalar
        def _(act):
            with act.Fori(0, B) as e:
                for cp in range(16):
                    act.wait_ge(sem["vps_ready"], e * 16 + (cp + 1))
                    act.activation(V[:, :, 2 * cp:2 * cp + 2].rearrange("a y c -> a c y"),
                                   PS[0:64, cp % 2, 0:2 * W].rearrange("a (c y) -> a c y", c=2), ACT.Copy)\
                       .then_inc(sem["vev_done"], 1)
                for n in range(2 * NQ):
                    act.wait_ge(sem["xt_ready"], e * 28 + (n + 1))
                    if n >= 2:
                        act.wait_ge(sem["f_ready"], e * 28 + (n - 1))
                    act.activation(XT[:, n % 2, :], PS[:, 2 + n % 2, :], ACT.Copy).then_inc(sem["xt_done"], 1)

        @block.vector
        def _(dve):
            steps = Steps(dve, sem["dve_step"])
            dve.wait_ge(sem["const_in"], 7 * 16)
            dve.wait_ge(sem["cst_in"], 1)
            steps.done(dve.tensor_tensor(cst[:], PS[0:1, 5, 0:B * C].rearrange("p (e c) -> p e c", c=C),
                                         bias[:].unsqueeze(1).to_broadcast([1, B, C]), ALU.add))
            steps.settle()
            steps.done(dve.tensor_scalar(cst[:], cst[:], float(W), None, ALU.mult))
            steps.settle()

            def modes(e):
                dve.wait_ge(sem["ys_in"], e * 32 + 32)
                dve.tensor_tensor(UT[0:1, 0, 0, 0:C], UT[0:1, 0, 0, 0:C], cst[:, bass.ds(e, 1), :].squeeze(1),
                                  ALU.add).then_inc(sem["ys_ready"], 1)

            def weights(e):
                after(dve, sem["f_ready"], e * 28)
                dve.tensor_scalar(Ws[:], Wbd[:], keep.acol1[:, bass.ds(e, 1)], None, ALU.mult)\
                   .then_inc(sem["w_ready"], 1)

            def body(e, prev, more):
                if prev is not None:
                    dve.wait_ge(sem["st_out"], prev * 2 + 1)
                    st.dve_deviations(dve, steps, ST, sem["st_in"])
                    dve.wait_ge(sem["st_out"], prev * 2 + 2)
                    st.dve_variance(dve, steps, ST, sem["root_in"])
                    dve.wait_ge(sem["root_out"], prev + 1)
                    st.dve_scales(dve, steps)
                    steps.done(dve.tensor_copy(keep.ab2[:, bass.ds(prev, 1), :].squeeze(1),
                                               st.ab[:].rearrange("p k g j -> p (k g j)")))
                if e is None:
                    return
                for n in range(2 * NQ):
                    q, t = divmod(n, T)
                    if n == 0:
                        after(dve, sem["stored"], e * 32)
                    dve.wait_ge(sem["f_ready"], e * 28 + (n + 1))
                    for ph in range(NP):
                        last = dve.scalar_tensor_tensor(
                            out=XO[:, t, ph, :, 4 * q:4 * q + 4].rearrange("p c y -> p y c"),
                            in0=PS[:, 4 + n % 2, :].rearrange("p (y k c) -> p k y c", c=C, k=NP)[:, ph], scalar=0.0,
                            in1=XC[:, q % RING, t].rearrange("p (y k c) -> p k y c", c=C, k=NP)[:, ph],
                            op0=ALU.max, op1=ALU.add)
                    last.then_inc(sem["f_done"], 1)
                    if more and n == 20:
                        modes(e + 1)
                if more:
                    weights(e + 1)
                dve.wait_ge(sem["f_done"], e * 28 + 28)
                for t in range(T):
                    for g in range(G):
                        last = dve.bn_stats(st.bn[:, t, g, :],
                                            XO[:, t, :, 2 * g:2 * g + 2, :].rearrange("p k c y -> p k (c y)"))
                last.then_inc(sem["st_in"], 1)

            modes(0)
            weights(0)
            turns(dve, body, steps, per_turn=keep.steps_c)


def pass_conv(nc, B, d, keep):
    R = H // 2
    NW = NB * NY
    with Scope(nc, "d_") as z:
        Bd = z.sb("Bd", [P, C * 3, P])
        X2 = z.sb("X2", [P, 4, NB, CG, NY])
        N2 = z.sb("N2", [P, 4, NB, NY + 2])
        Rl = z.sb("R", [P, 2, NW])
        X3 = z.sb("X3", [P, 2, NB, CG, NY])
        XR = z.sb("XR", [R, 2, T, NP, CG, NY])
        XP = z.sb("XP", [R, 2, CG, T, NP, NY])
        Zs = z.sb("Zs", [HALF, 2, P * C])
        SO = z.sb("SO", [P, 2, 512])
        Fr = z.sb("F", [R, T, P])
        Dc = z.sb("D", [HALF, 2, 64])
        rowstat = z.sb("rowstat", [R, 1, P])
        inside = z.sb("inside", [P, 2])
        b2 = z.sb("b2", [P, C])
        cf = z.sb("cf", [P, 3, 2, C])
        half = z.sb("half", [P, G])
        one = z.sb("one", [1, 1])
        rows4 = z.sb("rows4", [1, 2, P])
        st = GroupStats(z.sb, "st", T, W, rows=R)
        PS = z.ps("PS", [P, 8, 512])
        ST = PS[:, 7, :]
        names = ("const_in", "setup", "n2_ready", "conv_ready", "relu_ready", "x3_ready", "xp_ready",
                 "bn_read", "zps_ready", "zev_done", "modes_ready", "modes_out", "mst0", "mst1", "st_in", "st_out",
                 "root_in", "root_out", "dve_step")
        sem = {n: z.sem(n) for n in names}
        x2in = [z.sem(f"x2in{k}") for k in range(4)]
        x3in, x3out = ([z.sem(f"{s}{k}") for k in range(2)] for s in ("x3in", "x3out"))
        mst = (sem["mst0"], sem["mst1"])
        NCONST = 5
        bands_in = [z.sem(f"bands_in{k}") for k in range(2)]
        BANDS = (0, 12, C)
        row, sample2 = NP * C * NY, ROWS2 * NP * C * NY
        blocks = bass.AP(d["x2"].tensor, 0, [[sample2, B], [C * NY, NP], [row, 32], [RB * row, NB], [1, C * NY]])
        block = z.enter_context(nc.Block())

        def turns(engine, body, steps=None, per_turn=0):
            body(0, None, True)
            body(1, 0, True)
            with engine.Fori(2, B - 1) as e:
                if steps:
                    steps.enter(e - 2, per_turn)
                body(e, e - 1, True)
            if steps:
                steps.leave(B - 3)
            body(B - 1, B - 2, False)
            body(None, B - 1, False)

        @block.sync
        def _(sp):
            def load(e, cg):
                for ph in range(NP):
                    sp.dma_start(X2[32 * ph:32 * ph + 32, cg % 4].rearrange("r b c y -> r b (c y)"),
                                 blocks[e, ph, :, :, cg * CG * NY:(cg + 1) * CG * NY]).then_inc(x2in[cg % 4], 16)

            def store(e, cg):
                for ph in range(NP):
                    rows = slice(32 * ph + PADR, 32 * ph + PADR + RB)
                    sp.dma_start(d["x3"][e, :, ph, cg * CG:cg * CG + CG, :].rearrange("(b r) c y -> r b (c y)", r=RB),
                                 X3[rows, cg % 2].rearrange("r b c y -> r b (c y)")).then_inc(x3out[cg % 2], 16)

            def body(e, prev, more):
                if e is None:
                    return
                for cg in range(NCG):
                    sp.wait_ge(sem["x3_ready"], e * C + (cg + 1) * CG)
                    if cg < 4:
                        load(e, cg + 4)
                    elif more:
                        load(e + 1, cg - 4)
                    store(e, cg)

            for dst, src in ((Fr, d["F3"]), (Dc, d["D3"]), (rowstat, d["rowstat"]), (inside, d["inside"])):
                sp.dma_start(dst[:], src).then_inc(sem["const_in"], 16)
            sp.dma_start(b2[:], d["b2"].rearrange("(a c) -> a c", a=1).to_broadcast([P, C])).then_inc(sem["const_in"], 16)
            load(0, 0)
            bands = Bd[:].rearrange("p n m -> p (n m)")
            for k in range(2):
                cols = slice(BANDS[k] * 3 * P, BANDS[k + 1] * 3 * P)
                sp.dma_start(bands[:, cols], d["bands"][:, cols]).then_inc(bands_in[k], 16)
            for cg in range(1, 4):
                load(0, cg)
            turns(sp, body)
            for k in range(2):
                sp.wait_ge(x3out[k], B * 256)

        @block.gpsimd
        def _(pool):
            pool.memset(half[:], -0.5)
            pool.memset(one[:], 1.0)
            pool.memset(N2[:], 0.0).then_inc(sem["setup"], 1)
            pool.wait_ge(sem["setup"], 1)
            with pool.Fori(0, B) as e:
                pool.wait_ge(sem["root_in"], e + 1)
                pool.tensor_tensor(st.rs[:], st.var[:], half[:], ALU.pow).then_inc(sem["root_out"], 1)

        @block.tensor
        def _(pe):
            def conv(e, c):
                pe.wait_ge(sem["n2_ready"], e * C + (c + 1))
                after(pe, sem["relu_ready"], e * C + (c - 1))
                for s in range(3):
                    last = pe.matmul(PS[:, c % 2, 0:NW], Bd[:, c * 3 + s, :], N2[:, c % 4, :, s:s + NY],
                                     start=(s == 0), stop=(s == 2))
                last.then_inc(sem["conv_ready"], 1)

            def over_rows(e, cg):
                pe.wait_ge(sem["xp_ready"], e * NCG + (cg + 1))
                after(pe, sem["zev_done"], e * NCG + (cg - 1))
                for yc in range(2):
                    for k in range(CG):
                        for t in range(T):
                            last = pe.matmul(PS[0:HALF, 2 + 2 * (cg % 2) + yc, k * P:k * P + P],
                                             XP[:, cg % 2, k, t, 2 * yc:2 * yc + 2, :].rearrange("p k y -> p (k y)"),
                                             Fr[:, t, :], start=(t == 0), stop=(t == T - 1))
                last.then_inc(sem["zps_ready"], 1)

            def over_columns(e, quarter):
                if quarter == 0:
                    pe.wait_ge(sem["zev_done"], e * NCG + NCG)
                after(pe, sem["modes_out"], e * 4 + quarter)
                for j in range(8):
                    ap = 8 * quarter + j
                    for yc in range(2):
                        last = pe.matmul(PS[:, 6, j * 64:j * 64 + 64], Zs[:, yc, ap * P:ap * P + P], Dc[:, yc, :],
                                         start=(yc == 0), stop=(yc == 1))
                last.then_inc(sem["modes_ready"], 1)

            def body(e, prev, more):
                for c in range(C):
                    if prev is None and c in BANDS:
                        pe.wait_ge(bands_in[BANDS.index(c)], 16)
                    if e is not None:
                        conv(e, c)
                    if prev is None:
                        continue
                    if 5 <= c <= 26 and c % 3 == 2:
                        over_rows(prev, (c - 5) // 3)
                    if c == 27:
                        pe.wait_ge(sem["bn_read"], prev * NCG + NCG)
                        st.pe_mean(pe, ST, rowstat, lambda s: 0, sem["st_out"])
                    if c >= 28:
                        over_columns(prev, c - 28)
                    if c == 29:
                        pe.wait_ge(sem["st_in"], prev * 2 + 1)
                        st.pe_variance(pe, ST, rowstat, lambda s: 0, sem["st_out"])
                if prev is not None:
                    pe.wait_ge(sem["st_in"], prev * 2 + 2)
                    on_columns(pe, ST, rows4, one, sem["st_out"])

            pe.wait_ge(sem["const_in"], NCONST * 16)
            pe.wait_ge(sem["setup"], 1)
            turns(pe, body)

        @block.scalar
        def _(act):
            def reload(e, cg):
                after(act, sem["xp_ready"], e * NCG + (cg - 1))
                for t in range(T):
                    act.dma_start(XR[:, cg % 2, t].rearrange("p k c y -> p k (c y)"),
                                  d["x3"][e, t * R:t * R + R, :, cg * CG:cg * CG + CG, :]
                                  .rearrange("p k c y -> p k (c y)")).then_inc(x3in[cg % 2], 16)

            def by_channel(e, cg):
                act.wait_ge(x3in[cg % 2], e * 128 + (32 * (cg // 2) + 32))
                after(act, sem["zps_ready"], e * NCG + (cg - 1))
                after(act, sem["bn_read"], e * NCG + (cg - 1))
                for t in range(T):
                    last = act.activation(XP[:, cg % 2, :, t], XR[:, cg % 2, t].rearrange("p k c y -> p c k y"), ACT.Copy)
                last.then_inc(sem["xp_ready"], 1)

            def keep_rows_done(e, cg):
                if cg == 0:
                    after(act, sem["modes_ready"], e * 4)
                act.wait_ge(sem["zps_ready"], e * NCG + (cg + 1))
                for yc in range(2):
                    last = act.activation(Zs[:, yc].rearrange("p (q c) -> p c q", c=C)[:, CG * cg:CG * cg + CG, :],
                                          PS[0:HALF, 2 + 2 * (cg % 2) + yc, :].rearrange("p (c q) -> p c q", c=CG),
                                          ACT.Copy)
                last.then_inc(sem["zev_done"], 1)

            def keep_modes(e, quarter):
                k = quarter % 2
                act.wait_ge(sem["modes_ready"], e * 4 + (quarter + 1))
                after(act, mst[k], e * 32 + 16 * (quarter // 2))
                act.activation(SO[:, k, :], PS[:, 6, :], ACT.Copy).then_inc(sem["modes_out"], 1)
                act.wait_ge(sem["modes_out"], e * 4 + (quarter + 1))
                act.dma_start(d["spec3"][e, :, quarter * 512:quarter * 512 + 512], SO[:, k, :]).then_inc(mst[k], 16)

            def body(e, prev, more):
                for c in range(C):
                    if prev is not None:
                        if c == 1:
                            for k in range(2):
                                act.wait_ge(x3out[k], prev * 256 + 256)
                            reload(prev, 0)
                            reload(prev, 1)
                        if 4 <= c <= 25 and c % 3 == 1:
                            by_channel(prev, (c - 4) // 3)
                        if 6 <= c <= 27 and c % 3 == 0:
                            keep_rows_done(prev, (c - 6) // 3)
                        if 5 <= c <= 20 and c % 3 == 2:
                            reload(prev, (c - 5) // 3 + 2)
                        if c >= 29:
                            keep_modes(prev, c - 29)
                    if e is not None:
                        act.wait_ge(sem["conv_ready"], e * C + (c + 1))
                        after(act, sem["x3_ready"], e * C + (c - 1))
                        act.activation(Rl[:, c % 2], PS[:, c % 2, 0:NW], ACT.Relu, scale=2.25,
                                       bias=b2[:, c:c + 1]).then_inc(sem["relu_ready"], 1)
                if prev is not None:
                    keep_modes(prev, 3)

            act.wait_ge(sem["setup"], 2)
            turns(act, body)
            for k in range(2):
                act.wait_ge(mst[k], B * 32)

        @block.vector
        def _(dve):
            steps = Steps(dve, sem["dve_step"])
            dve.wait_ge(sem["const_in"], NCONST * 16)
            dve.wait_ge(sem["setup"], 1)
            dve.tensor_scalar(b2[:], b2[:], 2.25, None, ALU.mult).then_inc(sem["setup"], 1)

            def factors(e):
                steps.done(dve.tensor_copy(cf[:, 0].rearrange("p k c -> p (k c)"),
                                           keep.ab2[:, bass.ds(e, 1), :].squeeze(1)))
                steps.settle()
                for k in range(2):
                    last = dve.tensor_scalar(cf[:, 1 + k], cf[:, 0], inside[:, k:k + 1], None, ALU.mult)
                steps.done(last)
                steps.settle()

            def norm(e, c):
                cg, k = divmod(c, CG)
                if k == 0:
                    dve.wait_ge(x2in[cg % 4], e * 128 + (64 * (cg // 4) + 64))
                after(dve, sem["conv_ready"], e * C + (c - 3))
                for v, b0, b1 in ((1, 0, 1), (2, NB - 1, NB), (0, 1, NB - 1)):
                    last = dve.tensor_scalar(N2[:, c % 4, b0:b1, 1:1 + NY], X2[:, cg % 4, b0:b1, k, :],
                                             cf[:, v, 0, c:c + 1], cf[:, v, 1, c:c + 1], ALU.mult, ALU.add)
                last.then_inc(sem["n2_ready"], 1)

            def statistics(e, cg):
                dve.wait_ge(sem["xp_ready"], e * NCG + (cg + 1))
                for j in range(CG // 2):
                    for t in range(T):
                        last = dve.bn_stats(st.rows[:, t, cg * CG // 2 + j, :],
                                            XP[:, cg % 2, 2 * j:2 * j + 2, t].rearrange("p c k y -> p c (k y)"))
                last.then_inc(sem["bn_read"], 1)

            def body(e, prev, more):
                for c in range(C):
                    cg, k = divmod(c, CG)
                    if prev is not None:
                        if 5 <= c <= 26 and c % 3 == 2:
                            statistics(prev, (c - 5) // 3)
                        if c == 28:
                            dve.wait_ge(sem["st_out"], prev * 3 + 1)
                            st.dve_deviations(dve, steps, ST, sem["st_in"])
                        if c == 30:
                            dve.wait_ge(sem["st_out"], prev * 3 + 2)
                            st.dve_variance(dve, steps, ST, sem["root_in"])
                        if c == 31:
                            dve.wait_ge(sem["root_out"], prev + 1)
                            st.dve_scales(dve, steps)
                            for j in range(2):
                                last = dve.tensor_copy(rows4[0:1, j].rearrange("p (q c) -> p q c", c=C),
                                                       st.row(j)[0:1].unsqueeze(1).to_broadcast([1, 4, C]))
                            last.then_inc(sem["st_in"], 1)
                    if e is None:
                        continue
                    if c + 2 < C:
                        norm(e, c + 2)
                    elif more:
                        if c + 2 == C:
                            dve.wait_ge(sem["n2_ready"], e * C + C)
                            factors(e + 1)
                        norm(e + 1, c + 2 - C)
                    if k == 0:
                        after(dve, x3out[cg % 2], e * 256 + 64 * (cg // 2))
                    dve.wait_ge(sem["relu_ready"], e * C + (c + 1))
                    dve.tensor_tensor(X3[:, cg % 2, :, k, :], Rl[:, c % 2].rearrange("p (b y) -> p b y", y=NY),
                                      X2[:, cg % 4, :, k, :], ALU.add).then_inc(sem["x3_ready"], 1)
                if prev is not None:
                    dve.wait_ge(sem["st_out"], prev * 3 + 3)
                    steps.done(dve.tensor_copy(keep.acol3[:, bass.ds(prev, 1)], ST[:, 64:65]))
                    steps.done(dve.tensor_copy(keep.bcol3[:, bass.ds(prev, 1)], ST[:, 65:66]))

            factors(0)
            norm(0, 0)
            norm(0, 1)
            turns(dve, body, steps, per_turn=keep.steps_d)


def pass_inverse(nc, B, d, keep):
    R = H // 2
    with Scope(nc, "e_") as z:
        X3 = z.sb("X3", [R, 4, T, NP, CG, NY])
        OUT = z.sb("OUT", [R, 2, T, W, C])
        UT = z.sb("UT", [64, 2, 32, 2, 64])
        V = z.sb("V", [P, 4, 2 * W])
        Di = z.sb("Di", [64, W])
        Gr = z.sb("G", [P, T, R])
        PS = z.ps("PS", [P, 8, 512])
        names = ("const_in", "vps_ready", "vev_done", "f_ready", "f_done", "out0", "out1")
        sem = {n: z.sem(n) for n in names}
        xin = [z.sem(f"xin{k}") for k in range(4)]
        out_ = (sem["out0"], sem["out1"])
        ys_in = [z.sem(f"ys_in{k}") for k in range(2)]
        block = z.enter_context(nc.Block())

        @block.sync
        def _(sp):
            def load(e, cg):
                for t in range(T):
                    sp.dma_start(X3[:, cg % 4, t], d["x3"][e, t * R:t * R + R, :, cg * CG:cg * CG + CG, :])\
                      .then_inc(xin[cg % 4], 16)

            def load_modes(e, par):
                for h in range(2):
                    sp.dma_start(UT[:, par, :, h, :], d["y3"][e, h].rearrange("(a b) v -> b a v", b=64))\
                      .then_inc(ys_in[par], 16)

            def sample(e, par, more):
                for cg in range(NCG):
                    sp.wait_ge(sem["f_done"], e * 16 + (2 * cg + 2))
                    if cg == 0 and more:
                        load_modes(e + 1, 1 - par)
                    if cg < 4:
                        load(e, cg + 4)
                    elif more:
                        load(e + 1, cg - 4)

            for dst, src in ((Di, d["Di3"]), (Gr, d["G3"])):
                sp.dma_start(dst[:], src).then_inc(sem["const_in"], 16)
            load_modes(0, 0)
            for cg in range(4):
                load(0, cg)
            with sp.Fori(0, B // 2 - 1) as i:
                for par in range(2):
                    sample(i * 2 + par, par, True)
            for par in range(2):
                sample(B - 2 + par, par, par == 0)

        @block.tensor
        def _(pe):
            def over_columns(e16, par, cp):
                after(pe, sem["vev_done"], e16 + (cp - 1))
                for k in range(2):
                    last = pe.matmul(PS[:, 2 + cp % 2, k * W:k * W + W],
                                     UT[:, par].rearrange("b a h (q c) -> b (a h q) c", c=C)[:, :, 2 * cp + k], Di[:],
                                     start=True, stop=True)
                last.then_inc(sem["vps_ready"], 1)

            def over_rows(e16, cp):
                pe.wait_ge(sem["vev_done"], e16 + (cp + 1))
                after(pe, sem["f_done"], e16 + (cp - 1))
                for t in range(T):
                    last = pe.matmul(PS[0:R, 4 + 2 * (cp % 2) + t, 0:2 * W], Gr[:, t, :], V[:, cp % 4, :],
                                     start=True, stop=True)
                last.then_inc(sem["f_ready"], 1)

            def pair(i):
                for par in range(2):
                    e16 = i * 32 + 16 * par
                    pe.wait_ge(ys_in[par], i * 32 + 32)
                    over_columns(e16, par, 0)
                    over_columns(e16, par, 1)
                    for cp in range(16):
                        if cp + 2 < 16:
                            over_columns(e16, par, cp + 2)
                        over_rows(e16, cp)

            pe.wait_ge(sem["const_in"], 32)
            pair(0)
            with pe.Fori(1, B // 2) as i:
                pair(i)

        @block.scalar
        def _(act):
            def sample(e):
                for cp in range(16):
                    act.wait_ge(sem["vps_ready"], e * 16 + (cp + 1))
                    after(act, sem["f_ready"], e * 16 + (cp - 3))
                    act.activation(V[:, cp % 4, :], PS[:, 2 + cp % 2, 0:2 * W], ACT.Copy).then_inc(sem["vev_done"], 1)

            sample(0)
            with act.Fori(1, B) as e:
                sample(e)

        @block.vector
        def _(dve):
            def pair(i):
                for par in range(2):
                    e16 = i * 32 + 16 * par
                    after(dve, out_[par], i * 32)
                    for cp in range(16):
                        cg, k = divmod(cp, 2)
                        if k == 0:
                            dve.wait_ge(xin[cg % 4], i * 128 + (64 * par + 32 * (cg // 4) + 32))
                        dve.wait_ge(sem["f_ready"], e16 + (cp + 1))
                        for t in range(T):
                            for c in range(2):
                                last = dve.tensor_tensor(
                                    OUT[:, par, t, :, 2 * cp + c].rearrange("p (y k) -> p k y", k=NP),
                                    PS[0:R, 4 + 2 * (cp % 2) + t, c * W:c * W + W].rearrange("p (k y) -> p k y", k=NP),
                                    X3[:, cg % 4, t, :, 2 * k + c, :], ALU.add)
                        last.then_inc(sem["f_done"], 1)

            pair(0)
            with dve.Fori(1, B // 2) as i:
                pair(i)

        @block.gpsimd
        def _(pool):
            with pool.Fori(0, B // 2) as i:
                for par in range(2):
                    pool.wait_ge(sem["f_done"], i * 32 + (16 * par + 16))
                    for t in range(T):
                        pool.dma_start(d["out"][i * 2 + par, t * R:t * R + R], OUT[:, par, t]).then_inc(out_[par], 16)
            for par in range(2):
                pool.wait_ge(out_[par], (B // 2) * 32)


def tables():
    f = np.float64
    x = np.arange(H)
    rows = np.stack([ROW0[t] + np.arange(P) for t in range(T)])
    counts = np.zeros((T, P))
    for t in range(T):
        counts[t, ONCE[t]] = 1
    t = {}
    k = np.arange(P)[:, None]
    m = np.arange(P)[None, :]
    t["band"] = np.stack([(k >= m - (s // 2 - 1)) & (k <= m + s // 2) for s in SCALES], 1)
    for name, n in (("1", 32), ("3", 64)):
        hn = n // 2
        a = np.array([h * hn + ap for ap in range(hn) for h in range(2)], f)
        ang = 2 * np.pi * rows[:, :, None] * a / H
        fw = np.stack([np.cos(ang), -np.sin(ang)], -1).reshape(T, P, 2 * n) / np.sqrt(H)
        t["F" + name] = (fw * counts[:, :, None]).transpose(1, 0, 2)
        angs = 2 * np.pi * np.arange(H)[:, None] * a / H
        if name == "3":
            t["F3all"] = (np.stack([np.cos(angs), -np.sin(angs)], -1).reshape(T, H // 2, 2 * n)
                          / np.sqrt(H)).transpose(1, 0, 2)
        b = np.arange(n)[:, None]
        D = np.cos(np.pi * (x[None, :] + 0.5) * b / W) * np.where(b == 0, np.sqrt(1.0 / W), np.sqrt(2.0 / W))
        t["D" + name] = D.T.reshape(2, HALF, n).transpose(1, 0, 2)
        t["Di" + name] = D
        out_rows = rows if name == "1" else np.arange(H).reshape(T, H // 2)
        ang = 2 * np.pi * a[:, None, None] * out_rows[None] / H
        w = np.where(a == 0, 1.0, 2.0)[:, None, None] / np.sqrt(H)
        inv = np.stack([w * np.cos(ang), -w * np.sin(ang) * (a != 0)[:, None, None]], 1)
        t["G" + name] = inv.reshape(2 * n, T, -1)
    by_phase = np.arange(W).reshape(NY, NP).T.reshape(-1)
    t["D3"] = t["Di3"].T[by_phase].reshape(2, HALF, 64).transpose(1, 0, 2)
    t["Di3"] = t["Di3"][:, by_phase]
    t["F3"] = t["F3all"]
    del t["F3all"]
    block = np.arange(NB)[None, :] * RB - PADR + np.tile(np.arange(32), NP)[:, None]
    t["inside"] = ((block >= 0) & (block < H))[:, [0, NB - 1]]
    t["rowstat"] = np.full((H // 2, 1, P), ROWSTAT)
    once = np.broadcast_to(counts.T[:, :, None] * ROWSTAT, (P, T, P))
    t["once1"] = once
    t["ident"] = np.eye(P)
    return {key: np.ascontiguousarray(v, dtype=np.float32) for key, v in t.items()}


def mixing(Rr, Ri):
    n = Rr.shape[2]
    m = Rr.shape[3]
    re, im = (np.asarray(r).reshape(C, C, 2, n // 2, m).transpose(2, 1, 3, 4, 0) for r in (Rr, Ri))
    out = np.stack([np.concatenate([re, im], -1), np.concatenate([im, re], -1)], 1)
    return np.ascontiguousarray(out.reshape(P, n // 2 * m, 2 * C))


class Keep:
    pass


def program(nc, B, d):
    with Scope(nc, "k_") as z:
        keep = Keep()
        keep.steps_a, keep.steps_c, keep.steps_d = 198, 11, 14
        keep.acol1, keep.bcol1 = z.sb("acol1", [P, B]), z.sb("bcol1", [P, B])
        keep.acol3, keep.bcol3 = z.sb("acol3", [P, B]), z.sb("bcol3", [P, B])
        keep.ab2 = z.sb("ab2", [P, B, 2 * C])
        pass_fractal(nc, B, d, keep)
        mix_modes(nc, "b1_", B, 512, d, d["spec1"], d["y1"], d["R1"], keep.acol1, keep.bcol1)
        pass_spectral(nc, B, d, keep)
        pass_conv(nc, B, d, keep)
        mix_modes(nc, "b3_", B, 2048, d, d["spec3"], d["y3"], d["R3"], keep.acol3, keep.bcol3)
        pass_inverse(nc, B, d, keep)


def kernel(x, L0_conv_gamma, L0_conv_beta, L0_conv_moving_mean, L0_conv_moving_var, L1_conv_R_real, L1_conv_R_imag,
           L1_conv_W, L1_conv_b, L2_conv_W, L2_conv_b, L3_conv_R_real, L3_conv_R_imag):
    import concourse.bacc as bacc
    from concourse.bass_utils import run_bass_kernel_spmd

    B = x.shape[0]
    arrays = tables()
    arrays["x"] = np.ascontiguousarray(x)
    arrays["gamma"], arrays["beta"] = np.asarray(L0_conv_gamma), np.asarray(L0_conv_beta)
    arrays["mean"], arrays["var"] = np.asarray(L0_conv_moving_mean), np.asarray(L0_conv_moving_var)
    arrays["R1"] = mixing(L1_conv_R_real, L1_conv_R_imag)
    arrays["R3"] = mixing(L3_conv_R_real, L3_conv_R_imag)
    wt = np.ascontiguousarray(np.asarray(L1_conv_W).T)
    arrays["wt"] = wt
    wbd = np.zeros((P, P), np.float32)
    for k in range(4):
        wbd[k * C:k * C + C, k * C:k * C + C] = wt
    arrays["wbd"] = wbd
    arrays["b1"] = np.asarray(L1_conv_b).reshape(1, C)
    arrays["b2"] = np.asarray(L2_conv_b)
    w2 = np.asarray(L2_conv_W)[:, :, 0, :]
    bands = np.zeros((NP, 32, C, 3, NP, 32), np.float32)
    for dx in range(7):
        m = np.arange(3, 3 + RB)
        for pin in range(NP):
            for pout in range(NP):
                for s in range(3):
                    dy = 4 * (s - 1) + pin - pout + 3
                    if 0 <= dy < 7:
                        bands[pin, m + dx - 3, :, s, pout, m] = w2[dx, dy][None]
    arrays["bands"] = bands.reshape(P, -1)

    nc = bacc.Bacc("TRN2", target_bir_lowering=False, num_devices=1, dynamic_dma_scratch_size=4096)
    d = {}
    for name, a in arrays.items():
        d[name] = nc.dram_tensor("in_" + name, a.shape, mybir.dt.from_np(a.dtype), kind="ExternalInput").ap()
    for name, shape in (("x1", (B, H, W, C)), ("x2", (B, ROWS2, NP, C, NY)), ("x3", (B, ROWS3, NP, C, NY)),
                        ("spec1", (B, P, 512)), ("y1", (B, 2, 512, 64)), ("spec3", (B, P, 2048)), ("y3", (B, 2, 2048, 64))):
        d[name] = nc.dram_tensor("tmp_" + name, shape, F32).ap()
    d["out"] = nc.dram_tensor("out", (B, H, W, C), F32, kind="ExternalOutput").ap()
    program(nc, B, d)
    r = run_bass_kernel_spmd(nc, [{"in_" + k: v for k, v in arrays.items()}], core_ids=[0])
    return r.results[0]["out"]
```
